# Optimizing a Trainium2 kernel written in Bass

```python
import numpy as np
import jax
import jax.numpy as jnp

def _softmax(x, axis=-1):
    return jax.nn.softmax(x, axis=axis)

def _gelu(x):
    return jax.nn.gelu(x, approximate=True)

def _silu(x):
    return jax.nn.silu(x)

def _sigmoid(x):
    return jax.nn.sigmoid(x)

def _layernorm(x, axis=-1, eps=1e-05):
    m = jnp.mean(x, axis=axis, keepdims=True)
    v = jnp.var(x, axis=axis, keepdims=True)
    return (x - m) / jnp.sqrt(v + eps)

def _scatter_add(tgt, idx, src, axis=0):
    return tgt.at[idx].add(src)

def _segment_sum(src, seg, n):
    return jax.ops.segment_sum(src, seg, n)
kernel_name = 'mk_gnn_resnorm_d4_gnn_r32_336f22'

def setup_inputs(seed: int=0):
    np.random.seed(seed)
    _w = jnp.asarray

    def _rec_inputs():
        import jax
        import jax.numpy as jnp
        _gk = jax.random.key(seed)
        x = -0.0009044 + 1 * jax.random.normal(jax.random.fold_in(_gk, 1), (3125, 16), jnp.float32)
        _s = jax.random.randint(jax.random.fold_in(_gk, 2), (50000,), 0, 3125, jnp.int32)
        _d = jax.random.randint(jax.random.fold_in(_gk, 3), (50000,), 0, 3125, jnp.int32)
        _loop = jnp.arange(3125, dtype=jnp.int32)
        src = jnp.concatenate([_s, _d, _loop])
        dst = jnp.concatenate([_d, _s, _loop])
        _o = jnp.argsort(dst, stable=True)
        src = src[_o]
        dst = dst[_o]
        edge_attr_4 = 0.000714719 + 1.00021 * jax.random.normal(jax.random.fold_in(_gk, 11), (103125, 4), jnp.float32)
        edge_weight1 = jax.random.uniform(jax.random.fold_in(_gk, 13), (103125, 1), jnp.float32, 0.0, 1)
        node_vec1 = jax.random.uniform(jax.random.fold_in(_gk, 14), (3125, 1), jnp.float32, 0.0, 1)
        return (x, src, dst, edge_attr_4, edge_weight1, node_vec1)
    x, src, dst, edge_attr_4, edge_weight1, node_vec1 = _rec_inputs()

    def _L0_gnn_setup():
        import jax, jax.numpy as jnp
        import numpy as np
        N_NODES = 3125
        N_EDGES = 100000
        D_FEAT = 16
        key = jax.random.key(seed)
        kx, ke = jax.random.split(key)
        x = jax.random.normal(kx, (N_NODES, D_FEAT), dtype=jnp.float32)
        edge_index = jax.random.randint(ke, (2, N_EDGES), 0, N_NODES, dtype=jnp.int64)
        return {'x': x, 'edge_index': edge_index}
    _L0_gnn_all = _L0_gnn_setup()
    _L0_gnn_in = {k: v for k, v in _L0_gnn_all.items() if k in ()}
    del _L0_gnn_all

    def _L1_gnn_setup():
        import jax, jax.numpy as jnp
        import numpy as np
        STALK_DIM = 16
        N_NODES = 50000
        N_EDGES = 12500
        HIDDEN = 64
        key = jax.random.key(seed)
        k1, k2, k3, k4 = jax.random.split(key, 4)
        d = STALK_DIM
        x = jax.random.normal(k1, (N_NODES, d), dtype=jnp.float32)
        edge_index = jax.random.randint(k2, (2, N_EDGES), 0, N_NODES, dtype=jnp.int64)
        W1 = jax.random.normal(k3, (HIDDEN, 2 * d), dtype=jnp.float32) * (1.0 / np.sqrt(2 * d))
        b1 = jnp.zeros((HIDDEN,), dtype=jnp.float32)
        W2 = jax.random.normal(k4, (d, HIDDEN), dtype=jnp.float32) * (1.0 / np.sqrt(HIDDEN))
        b2 = jnp.zeros((d,), dtype=jnp.float32)
        return {'x': x, 'edge_index': edge_index, 'W1': W1, 'b1': b1, 'W2': W2, 'b2': b2}
    _L1_gnn_all = _L1_gnn_setup()
    _L1_gnn_in = {k: v for k, v in _L1_gnn_all.items() if k in ('W1', 'b1', 'W2', 'b2')}
    del _L1_gnn_all

    def _L2_gnn_setup():
        import jax, jax.numpy as jnp
        import numpy as np
        N_NODES = 3125
        N_EDGES = 100000
        FEAT = 16

        def gcn_conv(x, src, dst, W, b):
            n = x.shape[0]
            loop = jnp.arange(n, dtype=src.dtype)
            s = jnp.concatenate([src, loop])
            d = jnp.concatenate([dst, loop])
            deg = jax.ops.segment_sum(jnp.ones_like(d, dtype=x.dtype), d, num_segments=n)
            dinv = jnp.where(deg > 0, jax.lax.rsqrt(deg), 0.0)
            norm = dinv[s] * dinv[d]
            h = x @ W
            msg = h[s] * norm[:, None]
            out = jax.ops.segment_sum(msg, d, num_segments=n)
            return out + b
        key = jax.random.key(seed)
        k1, k2, k3, k4 = jax.random.split(key, 4)
        scale = 1.0 / np.sqrt(FEAT)
        return {'x': jax.random.normal(k1, (N_NODES, FEAT), dtype=jnp.float32), 'edge_index': jax.random.randint(k2, (2, N_EDGES), 0, N_NODES, dtype=jnp.int64) if jax.config.jax_enable_x64 else jax.random.randint(k2, (2, N_EDGES), 0, N_NODES, dtype=jnp.int32), 'W1': jax.random.normal(k3, (FEAT, 16), dtype=jnp.float32) * scale, 'b1': jnp.zeros((16,), dtype=jnp.float32), 'W2': jax.random.normal(k4, (16, FEAT), dtype=jnp.float32) * scale, 'b2': jnp.zeros((FEAT,), dtype=jnp.float32)}
    _L2_gnn_all = _L2_gnn_setup()
    _L2_gnn_in = {k: v for k, v in _L2_gnn_all.items() if k in ('W1', 'b1', 'W2', 'b2')}
    del _L2_gnn_all

    def _L3_gnn_setup():
        import jax, jax.numpy as jnp
        import numpy as np
        N, E = (50000, 25000)
        IN_NF, EDGE_NF, HID, OUT_NF, L = (16, 4, 128, 16, 4)

        def _lin(key, fan_in, fan_out):
            kw, kb = jax.random.split(key)
            bound = 1.0 / np.sqrt(fan_in)
            w = jax.random.uniform(kw, (fan_in, fan_out), jnp.float32, -bound, bound)
            b = jax.random.uniform(kb, (fan_out,), jnp.float32, -bound, bound)
            return (w, b)
        key = jax.random.key(seed)
        ks = jax.random.split(key, 16)
        h = jax.random.normal(ks[0], (N, IN_NF), jnp.float32)
        edge_index = jax.random.randint(ks[1], (2, E), 0, N, jnp.int32)
        edge_attr = jax.random.normal(ks[2], (E, EDGE_NF), jnp.float32)
        node_mask = jnp.ones((N, 1), jnp.float32)
        edge_mask = jnp.ones((E, 1), jnp.float32)
        emb_w, emb_b = _lin(ks[3], IN_NF, HID)
        out_w, out_b = _lin(ks[4], HID, OUT_NF)
        e1 = [_lin(jax.random.fold_in(ks[5], i), 2 * HID + EDGE_NF, HID) for i in range(L)]
        e2 = [_lin(jax.random.fold_in(ks[6], i), HID, HID) for i in range(L)]
        n1 = [_lin(jax.random.fold_in(ks[7], i), 2 * HID, HID) for i in range(L)]
        n2 = [_lin(jax.random.fold_in(ks[8], i), HID, HID) for i in range(L)]
        stk = lambda ps, j: jnp.stack([p[j] for p in ps])
        return {'h': h, 'edge_index': edge_index, 'edge_attr': edge_attr, 'node_mask': node_mask, 'edge_mask': edge_mask, 'emb_w': emb_w, 'emb_b': emb_b, 'edge_w1': stk(e1, 0), 'edge_b1': stk(e1, 1), 'edge_w2': stk(e2, 0), 'edge_b2': stk(e2, 1), 'node_w1': stk(n1, 0), 'node_b1': stk(n1, 1), 'node_w2': stk(n2, 0), 'node_b2': stk(n2, 1), 'out_w': out_w, 'out_b': out_b}
    _L3_gnn_all = _L3_gnn_setup()
    _L3_gnn_in = {k: v for k, v in _L3_gnn_all.items() if k in ('emb_w', 'emb_b', 'edge_w1', 'edge_b1', 'edge_w2', 'edge_b2', 'node_w1', 'node_b1', 'node_w2', 'node_b2', 'out_w', 'out_b')}
    del _L3_gnn_all
    return {'x': x, 'src': src, 'dst': dst, 'edge_attr_4': edge_attr_4, 'edge_weight1': edge_weight1, 'node_vec1': node_vec1, 'L1_gnn_W1': _L1_gnn_in['W1'], 'L1_gnn_b1': _L1_gnn_in['b1'], 'L1_gnn_W2': _L1_gnn_in['W2'], 'L1_gnn_b2': _L1_gnn_in['b2'], 'L2_gnn_W1': _L2_gnn_in['W1'], 'L2_gnn_b1': _L2_gnn_in['b1'], 'L2_gnn_W2': _L2_gnn_in['W2'], 'L2_gnn_b2': _L2_gnn_in['b2'], 'L3_gnn_emb_w': _L3_gnn_in['emb_w'], 'L3_gnn_emb_b': _L3_gnn_in['emb_b'], 'L3_gnn_edge_w1': _L3_gnn_in['edge_w1'], 'L3_gnn_edge_b1': _L3_gnn_in['edge_b1'], 'L3_gnn_edge_w2': _L3_gnn_in['edge_w2'], 'L3_gnn_edge_b2': _L3_gnn_in['edge_b2'], 'L3_gnn_node_w1': _L3_gnn_in['node_w1'], 'L3_gnn_node_b1': _L3_gnn_in['node_b1'], 'L3_gnn_node_w2': _L3_gnn_in['node_w2'], 'L3_gnn_node_b2': _L3_gnn_in['node_b2'], 'L3_gnn_out_w': _L3_gnn_in['out_w'], 'L3_gnn_out_b': _L3_gnn_in['out_b']}

def reference(x, src, dst, edge_attr_4, edge_weight1, node_vec1, L1_gnn_W1, L1_gnn_b1, L1_gnn_W2, L1_gnn_b2, L2_gnn_W1, L2_gnn_b1, L2_gnn_W2, L2_gnn_b2, L3_gnn_emb_w, L3_gnn_emb_b, L3_gnn_edge_w1, L3_gnn_edge_b1, L3_gnn_edge_w2, L3_gnn_edge_b2, L3_gnn_node_w1, L3_gnn_node_b1, L3_gnn_node_w2, L3_gnn_node_b2, L3_gnn_out_w, L3_gnn_out_b):
    import jax
    import jax.numpy as jnp

    def _L0_gnn_ref(x, edge_index):
        import jax, jax.numpy as jnp
        import numpy as np
        N_NODES = 3125
        N_EDGES = 100000
        D_FEAT = 16
        row = edge_index[0]
        col = edge_index[1]
        msg = jnp.take(x, col, axis=0)
        tmp = jnp.take(msg, col, axis=0)
        out = jax.ops.segment_sum(tmp, row, num_segments=x.shape[0])
        return out

    def _L1_gnn_ref(x, edge_index, W1, b1, W2, b2):
        import jax, jax.numpy as jnp
        import numpy as np
        STALK_DIM = 16
        N_NODES = 50000
        N_EDGES = 12500
        HIDDEN = 64
        d = x.shape[1]
        n = x.shape[0]
        src, dst = (edge_index[0], edge_index[1])
        xs, xd = (x[src], x[dst])

        def reflection(a, b):
            h = jax.nn.relu(jnp.concatenate([a, b], axis=1) @ W1.T + b1)
            return h @ W2.T + b2

        def householder(v):
            vn = v / jnp.maximum(jnp.linalg.norm(v, axis=1, keepdims=True), 1e-12)
            return jnp.eye(d, dtype=v.dtype)[None] - 2.0 * vn[:, :, None] * vn[:, None, :]
        F_s = householder(reflection(xs, xd))
        F_d = householder(reflection(xd, xs))
        L_sd = -jnp.einsum('eki,ekj->eij', F_s, F_d)
        ones_e = jnp.ones(src.shape[0], dtype=x.dtype)
        deg = jnp.zeros(n, dtype=x.dtype).at[src].add(ones_e).at[dst].add(ones_e)
        deg_inv_sqrt = 1.0 / jnp.sqrt(jnp.maximum(deg, 1e-05))
        coef = deg_inv_sqrt[src] * deg_inv_sqrt[dst]
        msg_s = coef[:, None] * jnp.einsum('eij,ej->ei', L_sd, xd)
        msg_d = coef[:, None] * jnp.einsum('eji,ej->ei', L_sd, xs)
        out = x - jnp.zeros_like(x).at[src].add(msg_s) - jnp.zeros_like(x).at[dst].add(msg_d)
        return jax.nn.relu(out)

    def _L2_gnn_ref(x, edge_index, W1, b1, W2, b2):
        import jax, jax.numpy as jnp
        import numpy as np
        N_NODES = 3125
        N_EDGES = 100000
        FEAT = 16

        def gcn_conv(x, src, dst, W, b):
            n = x.shape[0]
            loop = jnp.arange(n, dtype=src.dtype)
            s = jnp.concatenate([src, loop])
            d = jnp.concatenate([dst, loop])
            deg = jax.ops.segment_sum(jnp.ones_like(d, dtype=x.dtype), d, num_segments=n)
            dinv = jnp.where(deg > 0, jax.lax.rsqrt(deg), 0.0)
            norm = dinv[s] * dinv[d]
            h = x @ W
            msg = h[s] * norm[:, None]
            out = jax.ops.segment_sum(msg, d, num_segments=n)
            return out + b
        src, dst = (edge_index[0], edge_index[1])
        h = gcn_conv(x, src, dst, W1, b1)
        h = jax.nn.relu(h)
        out = gcn_conv(h, src, dst, W2, b2)
        return out

    def _L3_gnn_ref(h, edge_index, edge_attr, node_mask, edge_mask, emb_w, emb_b, edge_w1, edge_b1, edge_w2, edge_b2, node_w1, node_b1, node_w2, node_b2, out_w, out_b):
        import jax, jax.numpy as jnp
        import numpy as np
        N, E = (50000, 25000)
        IN_NF, EDGE_NF, HID, OUT_NF, L = (16, 4, 128, 16, 4)

        def _lin(key, fan_in, fan_out):
            kw, kb = jax.random.split(key)
            bound = 1.0 / np.sqrt(fan_in)
            w = jax.random.uniform(kw, (fan_in, fan_out), jnp.float32, -bound, bound)
            b = jax.random.uniform(kb, (fan_out,), jnp.float32, -bound, bound)
            return (w, b)
        row, col = (edge_index[0], edge_index[1])
        n = h.shape[0]
        h = h @ emb_w + emb_b
        for i in range(L):
            ef = jnp.concatenate([h[row], h[col], edge_attr], axis=1)
            ef = jax.nn.silu(ef @ edge_w1[i] + edge_b1[i])
            ef = jax.nn.silu(ef @ edge_w2[i] + edge_b2[i])
            ef = ef * edge_mask
            agg = jax.ops.segment_sum(ef, row, num_segments=n)
            nf = jnp.concatenate([h, agg], axis=1)
            nf = jax.nn.silu(nf @ node_w1[i] + node_b1[i])
            nf = nf @ node_w2[i] + node_b2[i]
            h = (h + nf) * node_mask
        out = (h @ out_w + out_b) * node_mask
        return out
    edge_index = jnp.stack([src, dst])
    x = _layernorm(x + _L0_gnn_ref(x, edge_index), axis=-1)
    x = _layernorm(x + _L1_gnn_ref(x, edge_index, L1_gnn_W1, L1_gnn_b1, L1_gnn_W2, L1_gnn_b2), axis=-1)
    x = _layernorm(x + _L2_gnn_ref(x, edge_index, L2_gnn_W1, L2_gnn_b1, L2_gnn_W2, L2_gnn_b2), axis=-1)
    x = _layernorm(x + _L3_gnn_ref(x, edge_index, edge_attr_4, node_vec1, edge_weight1, L3_gnn_emb_w, L3_gnn_emb_b, L3_gnn_edge_w1, L3_gnn_edge_b1, L3_gnn_edge_w2, L3_gnn_edge_b2, L3_gnn_node_w1, L3_gnn_node_b1, L3_gnn_node_w2, L3_gnn_node_b2, L3_gnn_out_w, L3_gnn_out_b), axis=-1)
    return x

_drawn_inputs = setup_inputs


def setup_inputs(seed=0):
    import zlib

    import numpy as np

    out = dict(_drawn_inputs(seed))
    spreads = {'L1_gnn_b1': (0.0, 0.701),
     'L1_gnn_b2': (0.0, 0.506),
     'L2_gnn_b1': (0.0, 0.1),
     'L2_gnn_b2': (0.0, 0.1)}
    factors = {'edge_attr_4': 8.0,
     'edge_weight1': 8.0,
     'L3_gnn_edge_b1': 8.0,
     'L3_gnn_edge_b2': 3.019,
     'L3_gnn_node_b1': 8.0,
     'L3_gnn_node_b2': 2.903,
     'L3_gnn_out_b': 6.313}
    for name, (base, spread) in spreads.items():
        noise = np.random.default_rng([zlib.crc32(name.encode()), seed]).standard_normal(out[name].shape)
        drawn = base * np.exp(spread * noise) if base else spread * noise
        out[name] = jnp.asarray(drawn.astype(out[name].dtype))
    for name, factor in factors.items():
        out[name] = (out[name] * factor).astype(out[name].dtype)
    return out
```

```python
import math
from contextlib import ExitStack

import numpy as np
import concourse.bass as bass
from concourse import mybir

F32 = mybir.dt.float32
BF16 = mybir.dt.bfloat16
I32 = mybir.dt.int32
ALU = mybir.AluOpType
ACT = mybir.ActivationFunctionType
AX = mybir.AxisListType.X

P = 128
N = 3125
E = 103125
F = 16
HID = 128
LAYERS = 4
EA = 4
R1 = 64
BN = 125
BLOCKS = N // BN
COLS = -(-E // P)
LASTROW = E - (P - 1) * COLS
SUBS = 2
TILE = SUBS * P
GROUP = 4
NS = GROUP * SUBS
TURNS = -(-((E + BLOCKS * (TILE - 1)) // TILE) // GROUP)
TILES = TURNS * GROUP
NSUB = TILES * SUBS
ROWC = NSUB + 1
PADSRC = 4000
SC_HALF = 13
SC_TURNS = COLS // (2 * SC_HALF)
W_DST, W_REL, W_VALID, W_EW, W_ATTR, W_DLO, W_DHI, PW = 0, 1, 2, 3, 4, 8, 9, 10
AP9 = 9 * EA
T1W = 2 * R1 + F + 1
EPS_LN = 1e-5
assert SC_TURNS * 2 * SC_HALF == COLS and BLOCKS * BN == N and NSUB % NS == 0


class Links:

    def __init__(self, eng, sem):
        self.eng, self.sem, self.n, self.base = eng, sem, 0, 0

    def __call__(self, ins):
        self.n += 1
        ins.then_inc(self.sem, 1)
        self.eng.wait_ge(self.sem, self.base + self.n)
        return ins


def split3(nc, link, parts, value, rest):
    link(nc.vector.tensor_copy(parts[0], value))
    link(nc.vector.tensor_tensor(rest, value, parts[0], ALU.subtract))
    link(nc.vector.tensor_copy(parts[1], rest))
    link(nc.vector.tensor_tensor(parts[2], rest, parts[1], ALU.subtract))


def split_rows(nc, link, out, value, row_masks, a, b, c, rest):
    split3(nc, link, (a, b, c), value, rest)
    link(nc.vector.tensor_scalar(out, a, row_masks[:, 0:1], None, ALU.mult))
    link(nc.vector.scalar_tensor_tensor(out, b, row_masks[:, 1:2], out, ALU.mult, ALU.add))
    link(nc.vector.scalar_tensor_tensor(out, c, row_masks[:, 2:3], out, ALU.mult, ALU.add))


def layer_norm(nc, link, out, x, sq, st):
    wide = [BN, BLOCKS, F]
    s, m, v = st[:, 0, :], st[:, 1, :], st[:, 2, :]
    link(nc.vector.tensor_reduce(s, x, AX, ALU.add))
    link(nc.vector.tensor_scalar(m, s, 1.0 / F, None, ALU.mult))
    link(nc.vector.tensor_tensor(out, x, m.unsqueeze(2).to_broadcast(wide), ALU.subtract))
    link(nc.vector.tensor_tensor(sq, out, out, ALU.mult))
    link(nc.vector.tensor_reduce(s, sq, AX, ALU.add))
    link(nc.vector.tensor_scalar(v, s, 1.0 / F, EPS_LN, ALU.mult, ALU.add))
    yield v
    link(nc.vector.reciprocal(m, v))
    link(nc.vector.tensor_tensor(out, out, m.unsqueeze(2).to_broadcast(wide), ALU.mult))


def gather_half(nc, gp, m, i, h, idx, rows, table, gathered, rows_used, idx_ready, tiles_before=0, halves_before=0):
    half = NS // 2
    for used in rows_used:
        gp.wait_ge(used, tiles_before + (i * GROUP + (2 * h + 2)))
    gp.sem_inc(m.pool_steps, 1)
    nc.gpsimd.tensor_copy(idx[:, h * half:(h + 1) * half],
                          m.meta[:, bass.ds(i * NS + h * half, half), W_DST].bitcast(I32)).then_inc(idx_ready, 1)
    gp.wait_ge(idx_ready, halves_before + (i * 2 + (h + 1)))
    gp.sem_inc(m.pool_steps, 1)
    for u in (2 * h, 2 * h + 1):
        for s in range(u * SUBS, (u + 1) * SUBS):
            gp.indirect_dma_start(rows[:, s, :], None, table,
                                  bass.IndirectOffsetOnAxis(ap=idx[:, s:s + 1], axis=0)).then_inc(gathered[u], 16)


def one_hots(nc, m, rec, src=None, dst_low=None, dst_high=None):
    for s in range(SUBS):
        if src is not None:
            last = nc.vector.tensor_scalar(src[:, s, :], m.iota[:, 0:BN], rec[:, s, W_REL:W_REL + 1],
                                           rec[:, s, W_VALID:W_VALID + 1], ALU.is_equal, ALU.mult)
        if dst_low is not None:
            last = nc.vector.tensor_scalar(dst_low[:, s, :], m.iota[:, 0:BN], rec[:, s, W_DLO:W_DLO + 1], None,
                                           ALU.is_equal)
        if dst_high is not None:
            last = nc.vector.tensor_scalar(dst_high[:, s, :], m.iota[:, 0:BLOCKS], rec[:, s, W_DHI:W_DHI + 1],
                                           rec[:, s, W_VALID:W_VALID + 1], ALU.is_equal, ALU.mult)
    return last


def flat(ap):
    return ap.rearrange("p o f -> p (o f)")


def block_of(eng, m, i, u):
    return eng.value_load(m.tile_block[0:1, bass.ds(i * GROUP + u, 1)], min_val=0, max_val=BLOCKS - 1)


class Mem:
    pass


class Stage(ExitStack):

    def __init__(self, name):
        super().__init__()
        self.name = name


def sb(nc, ctx, name, shape, dt=F32):
    return ctx.enter_context(nc.sbuf_tensor(f"{ctx.name}_{name}", shape, dt))


def bank(nc, ctx, name):
    return ctx.enter_context(nc.psum_tensor(f"{ctx.name}_{name}", [P, 512], F32))


def sems(nc, ctx, names):
    own = [ctx.enter_context(nc.semaphore(f"{ctx.name}_{n}")) for n in names.split()]

    def clear():
        nc.all_engine_barrier()
        for sem in own:
            nc.sync.sem_clear(sem)
        nc.all_engine_barrier()

    ctx.callback(clear)
    return own


def pool_dma_sems(nc, ctx, names):
    return tuple(nc.alloc_semaphore(f"{ctx.name}_{n}") for n in names.split())


def sort_edges(nc, m, src, dst, edge_attr, edge_w):
    NBK = BLOCKS + 1
    with Stage("sort_edges") as ctx:
        raw = sb(nc, ctx, "raw_index", [P, 2, COLS], I32)
        raw_w = sb(nc, ctx, "raw_weight", [P, COLS])
        raw_a = sb(nc, ctx, "raw_attr", [P, COLS * EA])
        srcf = sb(nc, ctx, "src_float", [P, COLS])
        dstf = sb(nc, ctx, "dst_float", [P, COLS])
        above = sb(nc, ctx, "above", [P, COLS])
        mask = sb(nc, ctx, "mask", [P, COLS])
        csum = sb(nc, ctx, "running_count", [P, COLS])
        place = sb(nc, ctx, "place", [P, COLS])
        hi_i = sb(nc, ctx, "place_high", [P, COLS], I32)
        lo_i = sb(nc, ctx, "place_low", [P, COLS], I32)
        row = sb(nc, ctx, "row", [P, COLS], I32)
        rec = sb(nc, ctx, "records", [P, COLS, PW])
        row_buf = sb(nc, ctx, "row_buf", [P, 2, SC_HALF], I32)
        rec_buf = sb(nc, ctx, "record_buf", [P, 2, SC_HALF, PW])
        cnt = sb(nc, ctx, "counts", [P, NBK])
        tri = sb(nc, ctx, "earlier_partition", [P, P])
        ones = sb(nc, ctx, "ones_square", [P, P])
        tot_i = sb(nc, ctx, "block_tiles_int", [P, NBK], I32)
        small = sb(nc, ctx, "small", [P, 6, NBK])
        tidx = sb(nc, ctx, "tile_number", [1, TILES])
        tblk = sb(nc, ctx, "tile_block_float", [1, TILES])
        zrow = sb(nc, ctx, "zero_rows", [P, ROWC])
        ps = bank(nc, ctx, "count_sums")
        (filled, loaded_src, loaded_dst, loaded_w, loaded_attr, const_step, const_ready, zeroed, counted, summed, dve_step,
         placed, copied, meta_in) = sems(
            nc, ctx, "filled loaded_src loaded_dst loaded_w loaded_attr const_step const_ready zeroed counted summed "
            "sort_step placed copied records_loaded")
        scattered = scat0, scat1 = pool_dma_sems(nc, ctx, "scattered0 scattered1")
        block = ctx.enter_context(nc.Block())
        cut = (P - 1) * COLS

        @block.sync
        def _(sp):
            sp.wait_ge(filled, 1)
            for k, (a, sem) in enumerate(((src, loaded_src), (dst, loaded_dst))):
                sp.dma_start(raw[0:P - 1, k, :], a[0:cut].rearrange("(p j) -> p j", p=P - 1)).then_inc(sem, 16)
                sp.dma_start(raw[P - 1:P, k, 0:LASTROW], a[cut:E].rearrange("(p j) -> p j", p=1)).then_inc(sem, 16)
            ew = edge_w.rearrange("e a -> (e a)")
            sp.dma_start(raw_w[0:P - 1, :], ew[0:cut].rearrange("(p j) -> p j", p=P - 1)).then_inc(loaded_w, 16)
            sp.dma_start(raw_w[P - 1:P, 0:LASTROW], ew[cut:E].rearrange("(p j) -> p j", p=1)).then_inc(loaded_w, 16)
            ea = edge_attr.rearrange("e a -> (e a)")
            sp.dma_start(raw_a[0:P - 1, :],
                         ea[0:cut * EA].rearrange("(p j) -> p j", p=P - 1)).then_inc(loaded_attr, 16)
            sp.dma_start(raw_a[P - 1:P, 0:LASTROW * EA],
                         ea[cut * EA:E * EA].rearrange("(p j) -> p j", p=1)).then_inc(loaded_attr, 16)
            zero_src = zrow[:, :]
            for w in range(PW):
                sp.dma_start(m.slots.rearrange("(p c) w -> p (c w)", p=P)[:, w * ROWC:(w + 1) * ROWC],
                             zero_src).then_inc(zeroed, 16)
            sp.wait_ge(scat0, 16 * SC_HALF * SC_TURNS)
            sp.wait_ge(scat1, 16 * SC_HALF * SC_TURNS)
            sp.dma_start(m.meta[:, :, :], m.slots.rearrange("(p c) w -> p c w", p=P)[:, 0:NSUB, :]).then_inc(meta_in, 16)
            sp.wait_ge(meta_in, 16)

        @block.gpsimd
        def _(gp):
            nc.gpsimd.memset(ones[:, :], 1.0).then_inc(const_step, 1)
            nc.gpsimd.memset(m.ident[:, :], 0.0).then_inc(const_step, 1)
            nc.gpsimd.memset(m.row_masks[:, :], 1.0).then_inc(const_step, 1)
            nc.gpsimd.iota(m.iota_i[:, :], [[1, P]], base=0, channel_multiplier=0).then_inc(const_step, 1)
            nc.gpsimd.iota(m.iota_t[:, :], [[1, TILES]], base=0, channel_multiplier=0).then_inc(const_step, 1)
            gp.wait_ge(const_step, 5)
            nc.gpsimd.affine_select(out=tri[:, :], in_=ones[:, :], compare_op=ALU.is_gt, fill=0.0, base=0,
                                    pattern=[[1, P]], channel_multiplier=-1).then_inc(const_ready, 1)
            nc.gpsimd.affine_select(out=m.ident[:, :], in_=m.ident[:, :], compare_op=ALU.not_equal, fill=1.0,
                                    base=0, pattern=[[-1, P]], channel_multiplier=1).then_inc(const_ready, 1)
            nc.gpsimd.affine_select(out=m.row_masks[:, :], in_=m.row_masks[:, :], compare_op=ALU.is_ge, fill=0.0,
                                    base=0, pattern=[[-3 * EA, 3]], channel_multiplier=1).then_inc(const_step, 1)
            gp.wait_ge(const_step, 6)
            nc.gpsimd.affine_select(out=m.row_masks[:, :], in_=m.row_masks[:, :], compare_op=ALU.is_ge, fill=0.0,
                                    base=3 * EA - 1, pattern=[[3 * EA, 3]],
                                    channel_multiplier=-1).then_inc(const_ready, 1)
            gp.wait_ge(zeroed, 16 * PW)
            with gp.Fori(0, SC_TURNS) as i:
                for h in range(2):
                    gp.wait_ge(copied, i * 2 + (h + 1))
                    gp.sem_inc(m.pool_steps, 1)
                    for j in range(SC_HALF):
                        gp.indirect_dma_start(m.slots, bass.IndirectOffsetOnAxis(ap=row_buf[:, h, j:j + 1], axis=0),
                                              rec_buf[:, h, j, :], None).then_inc(scattered[h], 16)

        @block.tensor
        def _(pe):
            pe.wait_ge(const_ready, 3)
            pe.wait_ge(counted, 1)
            nc.tensor.matmul(ps[:, 0:NBK], tri[:, :], cnt[:, :], start=True, stop=True)
            nc.tensor.matmul(ps[:, 64:64 + NBK], ones[:, :], cnt[:, :], start=True, stop=True).then_inc(summed, 1)

        @block.scalar
        def _(act):
            act.wait_ge(placed, 1)
            for h in range(2):
                c = h * SC_HALF
                nc.scalar.copy(rec_buf[:, h, :, :], rec[:, c:c + SC_HALF, :])
                nc.scalar.copy(row_buf[:, h, :], row[:, c:c + SC_HALF]).then_inc(copied, 1)
            with act.Fori(1, SC_TURNS) as i:
                for h in range(2):
                    act.wait_ge(scattered[h], i * (16 * SC_HALF))
                    c = i * (2 * SC_HALF) + h * SC_HALF
                    nc.scalar.copy(rec_buf[:, h, :, :], rec[:, bass.ds(c, SC_HALF), :])
                    nc.scalar.copy(row_buf[:, h, :], row[:, bass.ds(c, SC_HALF)]).then_inc(copied, 1)

        @block.vector
        def _(dve):
            link = Links(dve, dve_step)
            link(nc.vector.memset(raw[:, 0, :], PADSRC))
            link(nc.vector.memset(raw[:, 1, :], 0))
            link(nc.vector.memset(raw_w[:, :], 0.0))
            link(nc.vector.memset(raw_a[:, :], 0.0))
            nc.vector.memset(zrow[:, :], 0.0).then_inc(filled, 1)
            dve.wait_ge(loaded_src, 32)
            link(nc.vector.tensor_copy(srcf[:, :], raw[:, 0, :]))
            link(nc.vector.memset(place[:, :], 0.0))
            for b in range(NBK):
                link(nc.vector.tensor_scalar(above[:, :], srcf[:, :], float(BN * (b + 1)), None, ALU.is_ge))
                if b < BLOCKS:
                    link(nc.vector.scalar_tensor_tensor(mask[:, :], srcf[:, :], float(BN * b), above[:, :],
                                                        ALU.is_ge, ALU.subtract))
                else:
                    link(nc.vector.tensor_scalar(mask[:, :], srcf[:, :], float(BN * b), None, ALU.is_ge))
                link(nc.vector.tensor_tensor_scan(csum[:, :], mask[:, :], mask[:, :], 0.0, ALU.add, ALU.max))
                nc.vector.tensor_copy(cnt[:, b:b + 1], csum[:, COLS - 1:COLS])
                link(nc.vector.tensor_tensor(above[:, :], csum[:, :], mask[:, :], ALU.mult))
                link(nc.vector.tensor_tensor(place[:, :], place[:, :], above[:, :], ALU.add))
            nc.vector.tensor_scalar(place[:, :], place[:, :], -1.0, None, ALU.add).then_inc(counted, 1)
            dve.wait_ge(summed, 1)
            dve.wait_ge(const_ready, 3)
            tiles, start, base, step = (small[:, k, :] for k in range(4))
            link(nc.vector.tensor_scalar(tot_i[:, :], ps[:, 64:64 + NBK], float(TILE - 1), None, ALU.add))
            link(nc.vector.tensor_scalar(tot_i[:, :], tot_i[:, :], int(math.log2(TILE)), None,
                                         ALU.logical_shift_right))
            link(nc.vector.tensor_copy(tiles, tot_i[:, :]))
            link(nc.vector.memset(base, 0.0))
            link(nc.vector.tensor_tensor_scan(start, tiles, base, 0.0, ALU.add, ALU.add))
            link(nc.vector.tensor_tensor(start, start, tiles, ALU.subtract))
            link(nc.vector.memset(start[:, BLOCKS:NBK], float(TILES)))
            link(nc.vector.scalar_tensor_tensor(base, start, float(TILE), ps[:, 0:NBK], ALU.mult, ALU.add))
            link(nc.vector.tensor_copy(step[:, 0:1], base[:, 0:1]))
            link(nc.vector.tensor_tensor(step[:, 1:NBK], base[:, 1:NBK], base[:, 0:NBK - 1], ALU.subtract))
            link(nc.vector.tensor_scalar(place[:, :], place[:, :], step[:, 0:1], None, ALU.add))
            for b in range(1, NBK):
                link(nc.vector.tensor_scalar(above[:, :], srcf[:, :], float(BN * b), step[:, b:b + 1],
                                             ALU.is_ge, ALU.mult))
                link(nc.vector.tensor_tensor(place[:, :], place[:, :], above[:, :], ALU.add))
            link(nc.vector.tensor_copy(row[:, :], place[:, :]))
            link(nc.vector.tensor_scalar(hi_i[:, :], row[:, :], int(math.log2(P)), None, ALU.logical_shift_right))
            link(nc.vector.tensor_scalar(lo_i[:, :], row[:, :], P - 1, None, ALU.bitwise_and))
            link(nc.vector.scalar_tensor_tensor(row[:, :], lo_i[:, :], float(ROWC), hi_i[:, :], ALU.mult, ALU.add))
            for a, (w_lo, w_hi, idx, sem) in enumerate(((W_REL, None, 0, None), (W_DLO, W_DHI, 1, loaded_dst))):
                f = srcf if a == 0 else dstf
                if a == 1:
                    dve.wait_ge(loaded_dst, 32)
                    link(nc.vector.tensor_copy(dstf[:, :], raw[:, 1, :]))
                link(nc.vector.tensor_scalar(mask[:, :], f[:, :], float(BN), None, ALU.is_ge))
                for b in range(2, BLOCKS):
                    link(nc.vector.scalar_tensor_tensor(mask[:, :], f[:, :], float(BN * b), mask[:, :],
                                                        ALU.is_ge, ALU.add))
                link(nc.vector.scalar_tensor_tensor(rec[:, :, w_lo], mask[:, :], -float(BN), f[:, :],
                                                    ALU.mult, ALU.add))
                if w_hi is not None:
                    link(nc.vector.tensor_copy(rec[:, :, w_hi], mask[:, :]))
            link(nc.vector.tensor_copy(rec[:, :, W_DST].bitcast(I32), raw[:, 1, :]))
            link(nc.vector.tensor_scalar(rec[:, :, W_VALID], srcf[:, :], float(N), None, ALU.is_lt))
            dve.wait_ge(loaded_w, 32)
            link(nc.vector.tensor_copy(rec[:, :, W_EW], raw_w[:, :]))
            dve.wait_ge(loaded_attr, 32)
            nc.vector.tensor_copy(rec[:, :, W_ATTR:W_ATTR + EA],
                                  raw_a[:, :].rearrange("p (j a) -> p j a", a=EA)).then_inc(placed, 1)
            link(nc.vector.tensor_copy(m.iota[:, :], m.iota_i[:, :]))
            link(nc.vector.tensor_copy(tidx[:, :], m.iota_t[:, :]))
            link(nc.vector.tensor_scalar(tblk[:, :], tidx[:, :], start[0:1, 1:2], None, ALU.is_ge))
            for b in range(2, BLOCKS):
                link(nc.vector.scalar_tensor_tensor(tblk[:, :], tidx[:, :], start[0:1, b:b + 1], tblk[:, :],
                                                    ALU.is_ge, ALU.add))
            link(nc.vector.tensor_copy(m.tile_block[:, :], tblk[:, :]))
            link(nc.vector.memset(m.ones3[:, :], 1.0))


def first_pass(nc, m, x, dst):
    with Stage("first_pass") as ctx:
        yidx = sb(nc, ctx, "y_index", [BN, BLOCKS], I32)
        ynode = sb(nc, ctx, "y_node", [BN, BLOCKS, F + 1])
        idx = sb(nc, ctx, "index_buf", [P, NS], I32)
        yg = sb(nc, ctx, "y_gathered", [P, NS, F + 1])
        rec = sb(nc, ctx, "turn_records", [P, NS, PW])
        parts = sb(nc, ctx, "attr_parts", [P, NS, 3, 3, EA])
        a_hi = sb(nc, ctx, "attr_hi", [P, NS, EA], BF16)
        a_mid = sb(nc, ctx, "attr_mid", [P, NS, EA], BF16)
        a_lo = sb(nc, ctx, "attr_lo", [P, NS, EA], BF16)
        a_rest = sb(nc, ctx, "attr_rest", [P, NS, EA])
        oh = sb(nc, ctx, "one_hot_src", [P, NS, BN])
        dlo = sb(nc, ctx, "one_hot_dst_low", [P, NS, BN], BF16)
        dhi = sb(nc, ctx, "one_hot_dst_high", [P, NS, BLOCKS], BF16)
        ohT_sb = sb(nc, ctx, "one_hot_srcT", [BN, GROUP * TILE], BF16)
        atT_sb = sb(nc, ctx, "attr_partsT", [AP9, GROUP * TILE], BF16)
        zero = sb(nc, ctx, "zero_square", [P, P], BF16)
        psT = [bank(nc, ctx, f"one_hot_T_psum{k}") for k in range(2)]
        psA = [bank(nc, ctx, f"attr_T_psum{k}") for k in range(2)]
        psY = [bank(nc, ctx, f"sum_psum{k}") for k in range(2)]
        psD = bank(nc, ctx, "degree_psum")
        (yidx_in, y_out, idx_ready, tile_ready, attr_ready, transposed, copied,
         summed, added, stored0, stored1, half_free, dve_step, ones_set, deg_done, gates) = sems(
            nc, ctx, "yidx_in y_out idx_ready tile_ready attr_ready transposed "
            "copiedT summed added stored0 stored1 half_free pass_step ones_set deg_done gates")
        y_in, *gathered = pool_dma_sems(nc, ctx, "y_in gathered0 gathered1 gathered2 gathered3")
        stored = (stored0, stored1)
        block = ctx.enter_context(nc.Block())

        @block.sync
        def _(sp):
            sp.dma_start(yidx[:, :], dst[0:N].rearrange("(p b) -> p b", p=BN)).then_inc(yidx_in, 16)
            sp.dma_start(m.x[:, :, :], x.rearrange("(b p) f -> p b f", p=BN)).then_inc(m.x_in, 16)
            sp.wait_ge(y_in, 16 * BLOCKS)
            sp.wait_ge(ones_set, 1)
            sp.dma_start(m.ytab.rearrange("(p b) f -> p b f", p=BN), ynode[:, :, :]).then_inc(y_out, 16)
            sp.sem_inc(half_free, 2)
            with sp.Fori(0, TURNS) as i:
                for h in range(2):
                    sp.wait_ge(copied, i * GROUP + (2 * h + 2 + 2))
                    cols = slice(h * 2 * TILE, (h + 1) * 2 * TILE)
                    sp.dma_start(m.ohT[bass.ds(i, 1), :, cols].rearrange("o p c -> (o p) c"),
                                 ohT_sb[:, cols]).then_inc(stored[h], 16)
                    sp.dma_start(m.atT[bass.ds(i, 1), :, cols].rearrange("o p c -> (o p) c"),
                                 atT_sb[:, cols]).then_inc(stored[h], 16)
                for h in range(2):
                    sp.wait_ge(stored[h], i * 32 + 32)
                    sp.sem_inc(half_free, 1)

        @block.gpsimd
        def _(gp):
            gp.wait_ge(yidx_in, 16)
            gp.wait_ge(ones_set, 1)
            for b in range(BLOCKS):
                gp.indirect_dma_start(ynode[:, b, 0:F], None, x,
                                      bass.IndirectOffsetOnAxis(ap=yidx[:, b:b + 1], axis=0)).then_inc(y_in, 16)
            gp.wait_ge(y_out, 16)
            with gp.Fori(0, TURNS) as i:
                for h in range(2):
                    gather_half(nc, gp, m, i, h, idx, yg, m.ytab, gathered, (summed,), idx_ready)

        @block.vector
        def _(dve):
            link = Links(dve, dve_step)
            nc.vector.memset(ynode[:, :, F:F + 1], 1.0).then_inc(ones_set, 1)
            link(nc.vector.memset(zero[:, :], 0.0))
            link(nc.vector.memset(m.acc[:, :, :], 0.0))
            dve.sem_inc(added, 2)
            PER, first = 5, link.n

            def records(i):
                link.base, link.n = i * PER + first, 0
                dve.wait_ge(transposed, i * GROUP + 1)
                link(nc.vector.tensor_copy(rec[:, :, :], m.meta[:, i * NS:(i + 1) * NS, :] if isinstance(i, int)
                                           else m.meta[:, bass.ds(i * NS, NS), :]))
                split3(nc, link, (a_hi[:, :, :], a_mid[:, :, :], a_lo[:, :, :]), rec[:, :, W_ATTR:W_ATTR + EA],
                       a_rest[:, :, :])
                for k, part in enumerate((a_hi, a_mid, a_lo)):
                    last = nc.vector.tensor_copy(parts[:, :, :, k, :],
                                                 part[:, :, :].unsqueeze(2).to_broadcast([P, NS, 3, EA]))
                last.then_inc(attr_ready, 1)
                assert link.n == PER

            def build(i, u):
                dve.wait_ge(summed, i * GROUP + (u + 1))
                tile = slice(u * SUBS, (u + 1) * SUBS)
                one_hots(nc, m, rec[:, tile, :], oh[:, tile, :], dlo[:, tile, :], dhi[:, tile, :]).then_inc(tile_ready, 1)

            def add(i, u):
                blk = block_of(dve, m, i, u)
                dve.wait_ge(summed, i * GROUP + (u + 1 + GROUP))
                acc = flat(m.acc[:, bass.ds(blk, 1), :])
                nc.vector.tensor_tensor(acc, acc, psY[u % 2][0:BN, 0:F + 1], ALU.add).then_inc(added, 1)
                dve.wait_ge(added, i * GROUP + (u + 1 + 2))

            def turn(i, before):
                records(i)
                build(i, 0)
                if before is not None:
                    add(before, 2)
                build(i, 1)
                if before is not None:
                    add(before, 3)
                build(i, 2)
                add(i, 0)
                build(i, 3)
                add(i, 1)

            turn(0, None)
            dve.sem_inc(gates, 1)
            with dve.Fori(1, TURNS) as i:
                turn(i, i - 1)
            add(TURNS - 1, 2)
            add(TURNS - 1, 3)
            link.base, link.n = first + PER * TURNS, 0
            dve.wait_ge(deg_done, 1)
            link(nc.vector.tensor_copy(m.deg_dst[:, :], psD[0:BN, 0:BLOCKS]))

        @block.tensor
        def _(pe):
            pe.sem_inc(summed, GROUP)
            pe.sem_inc(transposed, 1)
            pe.wait_ge(dve_step, 2)
            nc.tensor.matmul(psD[0:BN, 0:BLOCKS], zero[:, 0:BN], zero[:, 0:BLOCKS], start=True, stop=False,
                             skip_group_check=True)
            with pe.Fori(0, TURNS) as i:
                pe.wait_ge(attr_ready, i + 1)
                for u in range(GROUP):
                    pe.wait_ge(tile_ready, i * GROUP + (u + 1))
                    pe.wait_ge(copied, i * GROUP + (u + 1))
                    for s in range(SUBS):
                        nc.tensor.transpose(psT[u % 2][0:BN, s * P:(s + 1) * P], oh[:, u * SUBS + s, :], m.ident[:, :])
                    for s in range(SUBS):
                        last = nc.tensor.transpose(psA[u % 2][0:AP9, s * P:(s + 1) * P],
                                                   parts[:, u * SUBS + s, :, :, :].rearrange("p l k a -> p (l k a)"),
                                                   m.ident[:, :])
                    last.then_inc(transposed, 1)
                    for s in range(SUBS):
                        nc.tensor.matmul(psD[0:BN, 0:BLOCKS], dlo[:, u * SUBS + s, :], dhi[:, u * SUBS + s, :],
                                         start=False, stop=False, skip_group_check=True)
                    pe.wait_ge(gathered[u], i * 32 + 32)
                    pe.wait_ge(added, i * GROUP + (u + 1))
                    for s in range(SUBS):
                        last = nc.tensor.matmul(psY[u % 2][0:BN, 0:F + 1], oh[:, u * SUBS + s, :],
                                                yg[:, u * SUBS + s, :], start=(s == 0), stop=(s == SUBS - 1))
                    last.then_inc(summed, 1)
            nc.tensor.matmul(psD[0:BN, 0:BLOCKS], zero[:, 0:BN], zero[:, 0:BLOCKS], start=False, stop=True,
                             skip_group_check=True).then_inc(deg_done, 1)

        @block.scalar
        def _(act):
            act.sem_inc(copied, 2)
            with act.Fori(0, TURNS) as i:
                for u in range(GROUP):
                    if u % 2 == 0:
                        act.wait_ge(half_free, i * 2 + (u // 2 + 1))
                    act.wait_ge(transposed, i * GROUP + (u + 2))
                    nc.scalar.copy(ohT_sb[:, u * TILE:(u + 1) * TILE], psT[u % 2][0:BN, 0:TILE])
                    nc.scalar.copy(atT_sb[:, u * TILE:(u + 1) * TILE], psA[u % 2][0:AP9, 0:TILE]).then_inc(copied, 1)


def norm_steps(nc, dve, link, m, x, sq, st, var_ready, root_ready):
    for _ in layer_norm(nc, link, x, x, sq, st):
        dve.sem_inc(var_ready, 1)
        dve.wait_ge(root_ready, 1)


def root(nc, act, st, var_ready, root_ready):
    act.wait_ge(var_ready, 1)
    nc.scalar.activation(st, st, ACT.Sqrt).then_inc(root_ready, 1)


def transpose_nodes(nc, pe, m, xo, width, banks, xT, transposed, copied):
    for k in range(-(-BLOCKS // 4)):
        if k >= 2:
            pe.wait_ge(copied, k - 1)
        for b in range(4 * k, min(4 * k + 4, BLOCKS)):
            last = nc.tensor.transpose(banks[k % 2][0:width, (b - 4 * k) * BN:(b - 4 * k + 1) * BN], xo[:, b, :],
                                       m.ident[0:BN, 0:BN])
        last.then_inc(transposed, 1)


def copy_transposed(nc, act, width, banks, xT, transposed, copied):
    for k in range(-(-BLOCKS // 4)):
        act.wait_ge(transposed, k + 1)
        n = min(4 * k + 4, BLOCKS) - 4 * k
        nc.scalar.copy(xT[0:width, 4 * k * BN:(4 * k + n) * BN], banks[k % 2][0:width, 0:n * BN]).then_inc(copied, 1)


def nodes_before_l1(nc, m, w):
    with Stage("nodes_before_l1") as ctx:
        sq = sb(nc, ctx, "squares", [BN, BLOCKS, F])
        st = sb(nc, ctx, "row_stats", [BN, 3, BLOCKS])
        deg = sb(nc, ctx, "degree", [BN, BLOCKS])
        xo = sb(nc, ctx, "x_and_one", [BN, BLOCKS, F + 1])
        xT = sb(nc, ctx, "xT", [F + 1, N])
        w1_sb = sb(nc, ctx, "w1_both", [F + 1, 4, R1])
        to_src = sb(nc, ctx, "rows_of_src", [BN, BLOCKS, T1W])
        to_dst = sb(nc, ctx, "rows_of_dst", [BN, BLOCKS, T1W])
        pT = [bank(nc, ctx, f"xT_psum{k}") for k in range(2)]
        pW = [bank(nc, ctx, f"project_psum{k}") for k in range(2)]
        (var_ready, root_ready, step, w_zero, w_in, bd_zero, bd_in, b2_in, x_ready, transposed, copied, projected, drained,
         deg_ready, deg_root, tab_ready, tab_out) = sems(
            nc, ctx, "var_ready root_ready norm_step w_zero w_in bd_zero bd_in b2_in x_ready xT_psum_ready xT_ready "
            "projected drained deg_ready deg_root table_ready table_out")
        block = ctx.enter_context(nc.Block())

        @block.sync
        def _(sp):
            sp.wait_ge(w_zero, 1)
            w1, b1, w2, b2 = w["L1_gnn_W1"], w["L1_gnn_b1"], w["L1_gnn_W2"], w["L1_gnn_b2"]
            with nc.allow_non_contiguous_dma(reason="a small weight, transposed"):
                for k, part in enumerate((0, 1, 1, 0)):
                    sp.dma_start(w1_sb[0:F, k, :], w1[:, part * F:(part + 1) * F].rearrange("h f -> f h")).then_inc(w_in, 16)
                for k in (0, 3):
                    sp.dma_start(w1_sb[F:F + 1, k, :], b1.rearrange("(o h) -> o h", o=1)).then_inc(w_in, 16)
                for k in range(2):
                    sp.dma_start(m.w2_pair[k * R1:(k + 1) * R1, k * F:(k + 1) * F],
                                 w2.rearrange("f h -> h f")).then_inc(bd_in, 16)
            for r in range(3):
                for k in range(2):
                    sp.dma_start(m.b2_rows[r:r + 1, k * F:(k + 1) * F],
                                 b2.rearrange("(o f) -> o f", o=1)).then_inc(b2_in, 16)
            sp.wait_ge(tab_ready, 1)
            sp.dma_start(m.tab1.rearrange("(b p) f -> p b f", p=BN), to_dst[:, :, :]).then_inc(tab_out, 16)
            sp.wait_ge(tab_out, 16)

        @block.gpsimd
        def _(gp):
            nc.gpsimd.memset(w1_sb[:, :, :], 0.0)
            nc.gpsimd.memset(m.w2_pair[:, :], 0.0).then_inc(w_zero, 1)

        @block.vector
        def _(dve):
            link = Links(dve, step)
            dve.wait_ge(m.x_in, 16)
            link(nc.vector.tensor_tensor(m.x[:, :, :], m.x[:, :, :], m.acc[:, :, 0:F], ALU.add))
            norm_steps(nc, dve, link, m, m.x[:, :, :], sq[:, :, :], st, var_ready, root_ready)
            link(nc.vector.memset(xo[:, :, :], 1.0))
            nc.vector.tensor_copy(xo[:, :, 0:F], m.x[:, :, :]).then_inc(x_ready, 1)
            link(nc.vector.tensor_tensor(deg[:, :], m.acc[:, :, F], m.deg_dst[:, :], ALU.add))
            nc.vector.tensor_scalar(deg[:, :], deg[:, :], 1e-5, None, ALU.max).then_inc(deg_ready, 1)
            dve.wait_ge(deg_root, 1)
            dve.wait_ge(x_ready, 1)
            link(nc.vector.reciprocal(deg[:, :], deg[:, :]))
            for t in (to_src, to_dst):
                nc.vector.tensor_copy(t[:, :, 2 * R1:2 * R1 + F], m.x[:, :, :])
                nc.vector.tensor_copy(t[:, :, 2 * R1 + F], deg[:, :])
            for b in range(BLOCKS):
                dve.wait_ge(projected, b + 1)
                nc.vector.tensor_copy(to_src[:, b, 0:2 * R1], pW[b % 2][0:BN, 0:2 * R1])
                ins = nc.vector.tensor_copy(to_dst[:, b, 0:2 * R1], pW[b % 2][0:BN, 2 * R1:4 * R1])
                ins.then_inc(drained, 1)
            dve.wait_ge(drained, BLOCKS)
            dve.sem_inc(tab_ready, 1)
            parts = tuple(m.rows1[:, :, k, :] for k in range(3))
            split3(nc, link, parts, to_src[:, :, :], to_src[:, :, :])
            dve.wait_ge(b2_in, 96)
            split_rows(nc, link, m.b2_parts[:, 0:2 * F], m.b2_rows[:, 0:2 * F], m.ident[0:3, 0:3],
                       *(m.b2_tmp[:, k, 0:2 * F] for k in range(3)), m.b2_rows[:, 0:2 * F])
            dve.wait_ge(bd_in, 32)

        @block.scalar
        def _(act):
            root(nc, act, st[:, 2, :], var_ready, root_ready)
            act.wait_ge(deg_ready, 1)
            nc.scalar.activation(deg[:, :], deg[:, :], ACT.Sqrt).then_inc(deg_root, 1)
            copy_transposed(nc, act, F + 1, pT, xT, transposed, copied)

        @block.tensor
        def _(pe):
            pe.wait_ge(x_ready, 1)
            transpose_nodes(nc, pe, m, xo, F + 1, pT, xT, transposed, copied)
            pe.wait_ge(w_in, 96)
            pe.wait_ge(copied, -(-BLOCKS // 4))
            for b in range(BLOCKS):
                if b >= 2:
                    pe.wait_ge(drained, b - 1)
                nc.tensor.matmul(pW[b % 2][0:BN, 0:4 * R1], xT[:, b * BN:(b + 1) * BN],
                                 w1_sb[:, :, :].rearrange("p k h -> p (k h)"), start=True, stop=True).then_inc(projected, 1)


def sheaf_edges(nc, m):
    PAIR = [P, NS, 2, F]
    with Stage("sheaf_edges") as ctx:
        idx = sb(nc, ctx, "index_buf", [P, NS], I32)
        rows = sb(nc, ctx, "rows_gathered", [P, NS, T1W])
        ohT = sb(nc, ctx, "one_hot_chunk", [BN, GROUP * TILE], BF16)
        rec = sb(nc, ctx, "turn_records", [P, NS, PW])
        hid = sb(nc, ctx, "hidden", [P, 2, TILE])
        xs = sb(nc, ctx, "x_src_dst", [P, NS, 2, F + 1])
        x_dst = sb(nc, ctx, "x_dst", [P, NS, F + 1])
        vu = sb(nc, ctx, "reflectors", [P, NS, 2, F])
        w = sb(nc, ctx, "reflected_once", [P, NS, 2, F])
        msg = sb(nc, ctx, "messages", [P, NS, 2, F])
        msg_src = sb(nc, ctx, "messages_to_src", [P, NS, F])
        prod = sb(nc, ctx, "products", [P, NS, 2, F])
        dots = sb(nc, ctx, "dots", [P, NS, 2])
        rcp = sb(nc, ctx, "two_over_norm", [P, NS, 2])
        coef = sb(nc, ctx, "coefficients", [P, NS])
        low = sb(nc, ctx, "dst_low", [P, NS])
        dist = sb(nc, ctx, "distance", [P, NS, BN])
        oh = sb(nc, ctx, "one_hot_src", [P, NS, BN])
        dlo = sb(nc, ctx, "one_hot_dst_low", [P, NS, BN])
        dhi = sb(nc, ctx, "one_hot_dst_high", [P, NS, BLOCKS])
        wide = sb(nc, ctx, "messages_by_block", [P, NS, BLOCKS, F])
        zero = sb(nc, ctx, "zero_square", [P, BLOCKS * F], BF16)
        psZ = [bank(nc, ctx, f"hidden_psum{k}") for k in range(2)]
        psV, psX = bank(nc, ctx, "reflector_psum"), bank(nc, ctx, "x_src_psum")
        psD = bank(nc, ctx, "node_sum_psum")
        (idx_ready, chunk0, chunk1, z_done, z_ready, hid_ready, hid_used, turn_in, x_in,
         math_done, math_step, tile_ready, summed, zeroed, d_done, act_step, low_ready) = sems(
            nc, ctx, "idx_ready chunk_in0 chunk_in1 z_done z_ready hid_ready hid_used "
            "turn_in x_dst_in math_done math_step tile_ready summed zeroed d_done act_step low_ready")
        gathered = pool_dma_sems(nc, ctx, "gathered0 gathered1 gathered2 gathered3")
        chunk_in = (chunk0, chunk1)
        block = ctx.enter_context(nc.Block())

        @block.sync
        def _(sp):
            load_chunks(nc, sp, m, ohT, chunk_in, z_done)

        @block.gpsimd
        def _(gp):
            with gp.Fori(0, TURNS) as i:
                for h in range(2):
                    gather_half(nc, gp, m, i, h, idx, rows, m.tab1, gathered, (z_done, x_in), idx_ready)

        @block.tensor
        def _(pe):
            pe.sem_inc(z_done, GROUP)
            pe.sem_inc(hid_used, 2)
            pe.sem_inc(summed, GROUP)
            pe.wait_ge(zeroed, 1)
            by_block = psD[0:BN, 0:BLOCKS * F].rearrange("p (b f) -> p b f", b=BLOCKS)
            nc.tensor.matmul(psD[0:BN, 0:BLOCKS * F], zero[:, 0:BN], zero[:, :], start=True, stop=False,
                             skip_group_check=True)

            def hidden(i, u):
                blk = block_of(pe, m, i, u)
                pe.wait_ge(hid_ready, i * GROUP + (u + 1))
                cols = slice(u * TILE, (u + 1) * TILE)
                if u % 2 == 0:
                    pe.wait_ge(chunk_in[u // 2], i * 16 + 16)
                for k in range(3):
                    nc.tensor.matmul(psZ[u % 2][:, 0:TILE], flat(m.rows1[:, bass.ds(blk, 1), k, 0:2 * R1]),
                                     ohT[:, cols], start=(k == 0), stop=False, skip_group_check=True)
                pe.wait_ge(gathered[u], i * 32 + 32)
                for s in range(SUBS):
                    last = nc.tensor.matmul(psZ[u % 2][:, s * P:(s + 1) * P], rows[:, u * SUBS + s, 0:2 * R1],
                                            m.ident[:, :], start=False, stop=(s == SUBS - 1), is_transpose=True,
                                            skip_group_check=True)
                last.then_inc(z_ready, 1)
                for s in range(u * SUBS, (u + 1) * SUBS):
                    for k in range(3):
                        last = nc.tensor.matmul(psX[:, s * (F + 1):(s + 1) * (F + 1)], ohT[:, s * P:(s + 1) * P],
                                                flat(m.rows1[:, bass.ds(blk, 1), k, 2 * R1:T1W]),
                                                start=(k == 0), stop=(k == 2))
                last.then_inc(z_done, 1)

            def reflectors(i, u):
                pe.wait_ge(hid_ready, i * GROUP + (u + 1 + 2))
                for s in range(SUBS):
                    out = psV[:, (u * SUBS + s) * 2 * F:(u * SUBS + s + 1) * 2 * F]
                    nc.tensor.matmul(out, m.ones3[:, :], m.b2_parts[:, 0:2 * F], start=True, stop=False)
                    last = nc.tensor.matmul(out, hid[:, u % 2, s * P:(s + 1) * P], m.w2_pair[:, :], start=False, stop=True)
                last.then_inc(hid_used, 1)

            def sums(i, u):
                blk = block_of(pe, m, i, u)
                pe.wait_ge(tile_ready, i * GROUP + (u + 1))
                pe.wait_ge(low_ready, i * GROUP + (u + 1))
                for s in range(u * SUBS, (u + 1) * SUBS):
                    nc.tensor.matmul(flat(by_block[:, bass.ds(blk, 1), :]), oh[:, s, :], msg_src[:, s, :],
                                     start=False, stop=False, skip_group_check=True)
                    last = nc.tensor.matmul(psD[0:BN, 0:BLOCKS * F], dlo[:, s, :],
                                            wide[:, s, :, :].rearrange("p b f -> p (b f)"),
                                            start=False, stop=False, skip_group_check=True)
                last.then_inc(summed, 1)

            def turn(i, summing):
                if summing is not None:
                    sums(summing, 0)
                    sums(summing, 1)
                pe.wait_ge(turn_in, i + 1)
                for u in range(GROUP):
                    hidden(i, u)
                    if summing is not None and u < 2:
                        sums(summing, u + 2)
                    if u:
                        reflectors(i, u - 1)
                reflectors(i, GROUP - 1)

            turn(0, None)
            turn(1, None)
            with pe.Fori(2, TURNS) as i:
                turn(i, i - 2)
            for i in (TURNS - 2, TURNS - 1):
                for u in range(GROUP):
                    sums(i, u)
            nc.tensor.matmul(psD[0:BN, 0:BLOCKS * F], zero[:, 0:BN], zero[:, :], start=False, stop=True,
                             skip_group_check=True).then_inc(d_done, 1)

        @block.scalar
        def _(act):
            act.sem_inc(hid_ready, 2)
            act.sem_inc(x_in, GROUP)
            act.sem_inc(turn_in, 1)

            def lows(i):
                nc.scalar.copy(low[:, :], m.meta[:, i * NS:(i + 1) * NS, W_DLO] if isinstance(i, int)
                               else m.meta[:, bass.ds(i * NS, NS), W_DLO]).then_inc(act_step, 1)
                act.wait_ge(act_step, i * (1 + GROUP) + 1)

            def one_hot_low(i, u):
                tile = slice(u * SUBS, (u + 1) * SUBS)
                for s in range(u * SUBS, (u + 1) * SUBS):
                    last = nc.scalar.activation(dist[:, s, :], m.iota[:, 0:BN], ACT.Abs, bias=low[:, s:s + 1], scale=-1.0)
                last.then_inc(act_step, 1)
                act.wait_ge(act_step, i * (1 + GROUP) + (u + 2))
                act.wait_ge(summed, i * GROUP + (u + 1))
                nc.scalar.activation(dlo[:, tile, :], dist[:, tile, :], ACT.Relu, bias=1.0, scale=-1.0).then_inc(low_ready, 1)

            def turn(i, before):
                if before is not None:
                    lows(before)
                for u in range(GROUP):
                    act.wait_ge(z_ready, i * GROUP + (u + 1))
                    act.wait_ge(hid_used, i * GROUP + (u + 1))
                    nc.scalar.activation(hid[:, u % 2, :], psZ[u % 2][:, 0:TILE], ACT.Relu).then_inc(hid_ready, 1)
                    if u == 0:
                        act.wait_ge(turn_in, i + 1)
                    act.wait_ge(gathered[u], i * 32 + 32)
                    tile = slice(u * SUBS, (u + 1) * SUBS)
                    nc.scalar.copy(x_dst[:, tile, :], rows[:, tile, 2 * R1:T1W]).then_inc(x_in, 1)
                    if before is not None:
                        one_hot_low(before, u)
                act.wait_ge(math_done, i + 1)
                act.wait_ge(x_in, i * GROUP + (GROUP + GROUP))
                nc.scalar.copy(xs[:, :, 1, :], x_dst[:, :, :])
                act.wait_ge(hid_used, i * GROUP + (GROUP + 2))
                act.wait_ge(z_done, i * GROUP + (GROUP + GROUP))
                nc.scalar.copy(xs[:, :, 0, :], psX[:, 0:NS * (F + 1)].rearrange("p (s f) -> p s f", s=NS))
                nc.scalar.copy(vu[:, :, :, :], psV[:, 0:NS * 2 * F].rearrange("p (s q f) -> p s q f", s=NS, q=2))\
                    .then_inc(turn_in, 1)

            turn(0, None)
            with act.Fori(1, TURNS) as i:
                turn(i, i - 1)
            lows(TURNS - 1)
            for u in range(GROUP):
                one_hot_low(TURNS - 1, u)

        @block.vector
        def _(dve):
            link = Links(dve, math_step)
            link(nc.vector.memset(zero[:, :], 0.0))
            dve.sem_inc(zeroed, 1)
            dve.sem_inc(math_done, 1)
            PER, first = 17, link.n
            tt, V = nc.vector.tensor_tensor, nc.vector

            def spread(a):
                return a.unsqueeze(3).to_broadcast(PAIR)

            def reflect(i):
                dve.wait_ge(turn_in, i + 2)
                link(tt(prod[:, :, :, :], vu[:, :, :, :], vu[:, :, :, :], ALU.mult))
                link(V.tensor_reduce(rcp[:, :, :], prod[:, :, :, :], AX, ALU.add))
                link(V.tensor_scalar(rcp[:, :, :], rcp[:, :, :], 1e-24, 0.5, ALU.max, ALU.mult))
                link(V.reciprocal(rcp[:, :, :], rcp[:, :, :]))
                link(tt(prod[:, :, :, :], vu[:, :, :, :], xs[:, :, :, 0:F], ALU.mult))
                link(V.tensor_reduce(dots[:, :, :], prod[:, :, :, :], AX, ALU.add))
                link(tt(dots[:, :, :], dots[:, :, :], rcp[:, :, :], ALU.mult))
                link(tt(prod[:, :, :, :], vu[:, :, :, :], spread(dots[:, :, :]), ALU.mult))
                for q in range(2):
                    last = tt(w[:, :, 1 - q, :], xs[:, :, q, 0:F], prod[:, :, q, :], ALU.subtract)
                link(last)
                link(tt(prod[:, :, :, :], vu[:, :, :, :], w[:, :, :, :], ALU.mult))
                link(V.tensor_reduce(dots[:, :, :], prod[:, :, :, :], AX, ALU.add))
                link(tt(dots[:, :, :], dots[:, :, :], rcp[:, :, :], ALU.mult))
                link(tt(prod[:, :, :, :], vu[:, :, :, :], spread(dots[:, :, :]), ALU.mult))
                tt(coef[:, :], xs[:, :, 0, F], xs[:, :, 1, F], ALU.mult)
                link(tt(w[:, :, :, :], w[:, :, :, :], prod[:, :, :, :], ALU.subtract))
                link(tt(msg[:, :, :, :], w[:, :, :, :],
                        coef[:, :].unsqueeze(2).unsqueeze(3).to_broadcast(PAIR), ALU.mult))
                dve.sem_inc(math_done, 1)
                link(V.tensor_copy(rec[:, :, :], m.meta[:, i * NS:(i + 1) * NS, :] if isinstance(i, int)
                                   else m.meta[:, bass.ds(i * NS, NS), :]))
                link(tt(dhi[:, :, :], m.iota[:, 0:BLOCKS].unsqueeze(1).to_broadcast([P, NS, BLOCKS]),
                        rec[:, :, W_DHI].unsqueeze(2).to_broadcast([P, NS, BLOCKS]), ALU.is_equal))

            def build(i, u):
                dve.wait_ge(summed, i * GROUP + (u + 1))
                tile = slice(u * SUBS, (u + 1) * SUBS)
                one_hots(nc, m, rec[:, tile, :], oh[:, tile, :])
                nc.vector.tensor_copy(msg_src[:, tile, :], msg[:, tile, 0, :])
                for s in range(u * SUBS, (u + 1) * SUBS):
                    last = tt(wide[:, s, :, :], dhi[:, s, :].unsqueeze(2).to_broadcast([P, BLOCKS, F]),
                              msg[:, s, 1, :].unsqueeze(1).to_broadcast([P, BLOCKS, F]), ALU.mult)
                last.then_inc(tile_ready, 1)

            def turn(i):
                link.base, link.n = i * PER + first, 0
                reflect(i)
                for u in range(GROUP):
                    build(i, u)
                assert link.n == PER, link.n

            turn(0)
            with dve.Fori(1, TURNS) as i:
                turn(i)
            link.base, link.n = first + PER * TURNS, 0
            dve.wait_ge(d_done, 1)
            link(nc.vector.tensor_copy(m.acc[:, :, 0:F],
                                       psD[0:BN, 0:BLOCKS * F].rearrange("p (b f) -> p b f", b=BLOCKS)))


def load_chunks(nc, sp, m, ohT, chunk_in, used, atT=None):
    with sp.Fori(0, TURNS) as i:
        for h in range(2):
            sp.wait_ge(used, i * GROUP + (2 * h + 2))
            cols = slice(h * 2 * TILE, (h + 1) * 2 * TILE)
            sp.dma_start(ohT[:, cols], m.ohT[bass.ds(i, 1), :, cols].rearrange("o p c -> (o p) c")).then_inc(chunk_in[h], 16)
            if atT is not None:
                sp.dma_start(atT[:, cols],
                             m.atT[bass.ds(i, 1), :, cols].rearrange("o p c -> (o p) c")).then_inc(chunk_in[h], 16)


def residual_norm(nc, m, name, add, relu=False):
    with Stage(name) as ctx:
        sq = sb(nc, ctx, "squares", [BN, BLOCKS, F])
        st = sb(nc, ctx, "row_stats", [BN, 3, BLOCKS])
        var_ready, root_ready, step = sems(nc, ctx, "var_ready root_ready norm_step")
        block = ctx.enter_context(nc.Block())

        @block.vector
        def _(dve):
            link = Links(dve, step)
            if relu:
                link(nc.vector.tensor_tensor(sq[:, :, :], m.x[:, :, :], add[:, :, 0:F], ALU.add))
                link(nc.vector.tensor_scalar(sq[:, :, :], sq[:, :, :], 0.0, None, ALU.max))
                link(nc.vector.tensor_tensor(m.x[:, :, :], m.x[:, :, :], sq[:, :, :], ALU.add))
            else:
                link(nc.vector.tensor_tensor(m.x[:, :, :], m.x[:, :, :], add[:, :, 0:F], ALU.add))
            norm_steps(nc, dve, link, m, m.x[:, :, :], sq[:, :, :], st, var_ready, root_ready)

        @block.scalar
        def _(act):
            root(nc, act, st[:, 2, :], var_ready, root_ready)


def conv_nodes_in(nc, m, name, w_dram, x_in):
    with Stage(name) as ctx:
        wt = sb(nc, ctx, "weight", [F, F])
        xT = sb(nc, ctx, "xT", [F, N])
        rest = sb(nc, ctx, "rest", [BN, BLOCKS, F])
        pT = [bank(nc, ctx, f"xT_psum{k}") for k in range(2)]
        pW = bank(nc, ctx, "project_psum")
        w_in, deg_ready, deg_root, transposed, copied, projected, step = sems(
            nc, ctx, "w_in deg_ready deg_root xT_psum_ready xT_ready projected step")
        block = ctx.enter_context(nc.Block())

        @block.sync
        def _(sp):
            sp.dma_start(wt[:, :], w_dram).then_inc(w_in, 16)

        @block.tensor
        def _(pe):
            transpose_nodes(nc, pe, m, x_in, F, pT, xT, transposed, copied)
            pe.wait_ge(w_in, 16)
            pe.wait_ge(copied, -(-BLOCKS // 4))
            for b in range(BLOCKS):
                last = nc.tensor.matmul(pW[0:BN, b * F:(b + 1) * F], xT[:, b * BN:(b + 1) * BN], wt[:, :],
                                        start=True, stop=True)
            last.then_inc(projected, 1)

        @block.scalar
        def _(act):
            act.wait_ge(deg_ready, 1)
            nc.scalar.activation(m.dinv[:, :], m.dinv[:, :], ACT.Sqrt).then_inc(deg_root, 1)
            copy_transposed(nc, act, F, pT, xT, transposed, copied)

        @block.vector
        def _(dve):
            link = Links(dve, step)
            nc.vector.tensor_scalar(m.dinv[:, :], m.deg_dst[:, :], 1.0, None, ALU.add).then_inc(deg_ready, 1)
            dve.wait_ge(deg_root, 1)
            link(nc.vector.reciprocal(m.dinv[:, :], m.dinv[:, :]))
            dve.wait_ge(projected, 1)
            link(nc.vector.tensor_tensor(m.scaled[:, :, :], pW[0:BN, 0:BLOCKS * F].rearrange("p (b f) -> p b f", b=BLOCKS),
                                         m.dinv[:, :].unsqueeze(2).to_broadcast([BN, BLOCKS, F]), ALU.mult))
            split3(nc, link, tuple(m.rows2[:, :, k, :] for k in range(3)), m.scaled[:, :, :], rest[:, :, :])


def conv_edges(nc, m, name, b_dram, out, last_conv):
    with Stage(name) as ctx:
        ohT = sb(nc, ctx, "one_hot_chunk", [BN, GROUP * TILE], BF16)
        low = sb(nc, ctx, "dst_low", [P, NS])
        high = sb(nc, ctx, "dst_high", [P, NS])
        dlo = sb(nc, ctx, "one_hot_dst_low", [P, NS, BN])
        dhi = sb(nc, ctx, "one_hot_dst_high", [P, NS, BLOCKS])
        wide = sb(nc, ctx, "rows_by_block", [P, NS, BLOCKS, F])
        zero = sb(nc, ctx, "zero_square", [P, BLOCKS * F], BF16)
        bias = sb(nc, ctx, "bias", [BN, F])
        psG = [bank(nc, ctx, f"row_psum{k}") for k in range(2)]
        psD = bank(nc, ctx, "sum_psum")
        (b_in, chunk0, chunk1, low_step, hot_ready, fetched, spread_done, summed, zeroed, d_done, step) = sems(
            nc, ctx, "b_in chunk_in0 chunk_in1 low_step hot_ready fetched spread_done summed zeroed d_done step")
        chunk_in = (chunk0, chunk1)
        block = ctx.enter_context(nc.Block())

        @block.sync
        def _(sp):
            sp.dma_start(bias[:, :], b_dram.rearrange("(o f) -> o f", o=1).to_broadcast([BN, F])).then_inc(b_in, 16)
            load_chunks(nc, sp, m, ohT, chunk_in, fetched)

        @block.gpsimd
        def _(gp):
            with gp.Fori(0, TURNS) as i:
                for h in range(2):
                    gp.wait_ge(summed, i * GROUP + (2 * h + 2))
                    gp.sem_inc(m.pool_steps, 1)
                    half = slice(h * NS // 2, (h + 1) * NS // 2)
                    nc.gpsimd.tensor_copy(low[:, half], m.meta[:, bass.ds(i * NS + h * (NS // 2), NS // 2), W_DLO])\
                        .then_inc(low_step, 1)
                    gp.wait_ge(low_step, i * 2 + (h + 1))
                    gp.sem_inc(m.pool_steps, 1)
                    for u in (2 * h, 2 * h + 1):
                        for s in range(u * SUBS, (u + 1) * SUBS):
                            last = nc.gpsimd.tensor_scalar(dlo[:, s, :], m.iota[:, 0:BN], low[:, s:s + 1], None, ALU.is_equal)
                        last.then_inc(hot_ready, 1)

        @block.tensor
        def _(pe):
            pe.sem_inc(fetched, GROUP)
            pe.sem_inc(summed, GROUP)
            pe.wait_ge(zeroed, 1)
            nc.tensor.matmul(psD[0:BN, 0:BLOCKS * F], zero[:, 0:BN], zero[:, :], start=True, stop=False,
                             skip_group_check=True)

            def fetch(i, u):
                blk = block_of(pe, m, i, u)
                pe.wait_ge(spread_done, i * GROUP + (u + 1))
                if u % 2 == 0:
                    pe.wait_ge(chunk_in[u // 2], i * 16 + 16)
                for s in range(SUBS):
                    for k in range(3):
                        c = (u * SUBS + s) * P
                        last = nc.tensor.matmul(psG[u % 2][:, s * F:(s + 1) * F], ohT[:, c:c + P],
                                                flat(m.rows2[:, bass.ds(blk, 1), k, :]), start=(k == 0), stop=(k == 2))
                last.then_inc(fetched, 1)

            def sums(i, u):
                pe.wait_ge(spread_done, i * GROUP + (u + 1 + 2))
                pe.wait_ge(hot_ready, i * GROUP + (u + 1))
                for s in range(SUBS):
                    last = nc.tensor.matmul(psD[0:BN, 0:BLOCKS * F], dlo[:, u * SUBS + s, :],
                                            wide[:, u * SUBS + s, :, :].rearrange("p b f -> p (b f)"),
                                            start=False, stop=False, skip_group_check=True)
                last.then_inc(summed, 1)

            for u in range(GROUP):
                fetch(0, u)
                if u:
                    sums(0, u - 1)
            with pe.Fori(1, TURNS) as i:
                for u in range(GROUP):
                    fetch(i, u)
                    sums(i if u else i - 1, (u - 1) % GROUP)
            sums(TURNS - 1, GROUP - 1)
            nc.tensor.matmul(psD[0:BN, 0:BLOCKS * F], zero[:, 0:BN], zero[:, :], start=False, stop=True,
                             skip_group_check=True).then_inc(d_done, 1)

        @block.vector
        def _(dve):
            link = Links(dve, step)
            nc.vector.memset(zero[:, :], 0.0).then_inc(zeroed, 1)
            dve.sem_inc(spread_done, 2)
            with dve.Fori(0, TURNS) as i:
                link.base, link.n = i * 2, 0
                link(nc.vector.tensor_copy(high[:, :], m.meta[:, bass.ds(i * NS, NS), W_DHI]))
                link(nc.vector.tensor_tensor(dhi[:, :, :], m.iota[:, 0:BLOCKS].unsqueeze(1).to_broadcast([P, NS, BLOCKS]),
                                             high[:, :].unsqueeze(2).to_broadcast([P, NS, BLOCKS]), ALU.is_equal))
                for u in range(GROUP):
                    dve.wait_ge(fetched, i * GROUP + (u + 1 + GROUP))
                    dve.wait_ge(summed, i * GROUP + (u + 1))
                    for s in range(SUBS):
                        last = nc.vector.tensor_tensor(
                            wide[:, u * SUBS + s, :, :],
                            psG[u % 2][:, s * F:(s + 1) * F].unsqueeze(1).to_broadcast([P, BLOCKS, F]),
                            dhi[:, u * SUBS + s, :].unsqueeze(2).to_broadcast([P, BLOCKS, F]), ALU.mult)
                    last.then_inc(spread_done, 1)
            link.base, link.n = 2 * TURNS, 0
            dve.wait_ge(d_done, 1)
            dve.wait_ge(b_in, 16)
            full = [BN, BLOCKS, F]
            link(nc.vector.tensor_tensor(out[:, :, :], psD[0:BN, 0:BLOCKS * F].rearrange("p (b f) -> p b f", b=BLOCKS),
                                         m.scaled[:, :, :], ALU.add))
            link(nc.vector.tensor_tensor(out[:, :, :], out[:, :, :], m.dinv[:, :].unsqueeze(2).to_broadcast(full), ALU.mult))
            link(nc.vector.tensor_tensor(out[:, :, :], out[:, :, :], bias[:, :].unsqueeze(1).to_broadcast(full), ALU.add))
            if not last_conv:
                link(nc.vector.tensor_scalar(out[:, :, :], out[:, :, :], 0.0, None, ALU.max))


CHUNK = 500
CHUNKS = [(c, min(CHUNK, N - c)) for c in range(0, N, CHUNK)]


def embed(nc, m, w):
    with Stage("embed") as ctx:
        wt = sb(nc, ctx, "weight", [F, HID])
        bt = sb(nc, ctx, "bias", [HID, 1])
        xT = sb(nc, ctx, "xT", [F, N])
        pT = [bank(nc, ctx, f"xT_psum{k}") for k in range(2)]
        pH = [bank(nc, ctx, f"h_psum{k}") for k in range(2)]
        w_in, transposed, copied, projected, stored = sems(nc, ctx, "w_in xT_psum_ready xT_ready projected stored")
        block = ctx.enter_context(nc.Block())

        @block.sync
        def _(sp):
            sp.dma_start(wt[:, :], w["L3_gnn_emb_w"]).then_inc(w_in, 16)
            sp.dma_start(bt[:, :], w["L3_gnn_emb_b"].rearrange("(h o) -> h o", o=1)).then_inc(w_in, 16)
            sp.dma_start(m.node_mask[:, :], w["node_vec1"].rearrange("n o -> o n").to_broadcast([HID, N])).then_inc(w_in, 16)

        @block.tensor
        def _(pe):
            transpose_nodes(nc, pe, m, m.x, F, pT, xT, transposed, copied)
            pe.wait_ge(w_in, 48)
            pe.wait_ge(copied, -(-BLOCKS // 4))
            for k, (c, n) in enumerate(CHUNKS):
                if k >= 2:
                    pe.wait_ge(stored, k - 1)
                nc.tensor.matmul(pH[k % 2][:, 0:n], wt[:, :], xT[:, c:c + n], start=True, stop=True).then_inc(projected, 1)

        @block.scalar
        def _(act):
            copy_transposed(nc, act, F, pT, xT, transposed, copied)

        @block.vector
        def _(dve):
            for k, (c, n) in enumerate(CHUNKS):
                dve.wait_ge(projected, k + 1)
                nc.vector.tensor_scalar(m.h[:, c:c + n], pH[k % 2][:, 0:n], bt[:, 0:1], None, ALU.add).then_inc(stored, 1)


def egnn_layers(nc, m, w):
    W_DMAS = 8 + 9 + 3
    with Stage("egnn") as ctx:
        w_ab = sb(nc, ctx, "edge_w1_nodes", [HID, 2, HID])
        w_c = sb(nc, ctx, "edge_w1_attr", [AP9, HID])
        wc_tmp = sb(nc, ctx, "edge_w1_attr_whole_parts", [AP9, 3, HID], BF16)
        wc_parts = sb(nc, ctx, "edge_w1_attr_parts", [AP9, HID], BF16)
        w_2 = sb(nc, ctx, "edge_w2", [HID, HID])
        n_1 = sb(nc, ctx, "node_w1", [HID, 2, HID])
        n_2 = sb(nc, ctx, "node_w2", [HID, HID])
        biases = sb(nc, ctx, "biases", [HID, 3])
        rows = sb(nc, ctx, "rows_of_src_parts", [BN, BLOCKS, 3, HID], BF16)
        rest = sb(nc, ctx, "rest", [BN, HID])
        q_sb = sb(nc, ctx, "rows_of_dst", [BN, BLOCKS, HID])
        agg = sb(nc, ctx, "sums", [HID, N])
        n_hid = sb(nc, ctx, "node_hidden", [HID, 2, CHUNK])
        idx = sb(nc, ctx, "index_buf", [P, NS], I32)
        q_got = sb(nc, ctx, "rows_gathered", [P, NS, HID])
        ohT = sb(nc, ctx, "one_hot_chunk", [BN, GROUP * TILE], BF16)
        atT = sb(nc, ctx, "attr_chunk", [AP9, GROUP * TILE], BF16)
        rec = sb(nc, ctx, "turn_records", [P, NS, PW])
        hid = sb(nc, ctx, "hidden", [HID, 2, TILE])
        ef = sb(nc, ctx, "edge_features", [P, 2, SUBS, HID])
        oh = sb(nc, ctx, "one_hot_weighted", [P, 2 * SUBS, BN])
        psZ = [bank(nc, ctx, f"hidden_psum{k}") for k in range(2)]
        psY = [bank(nc, ctx, f"feature_psum{k}") for k in range(2)]
        psS = [bank(nc, ctx, f"sum_psum{k}") for k in range(2)]
        (w_in, w_split, projected, q_projected, kept, q_kept, q_out, layer_done, idx_ready, chunk0, chunk1, z_done,
         hid_ready, hid_used, ef_ready, summed, added, hot_ready, edges_done, n1_done, n_silu, n2_done, updated, step, gates) = sems(
            nc, ctx, "w_in w_split projected q_projected kept q_kept q_out layer_done idx_ready chunk_in0 "
            "chunk_in1 z_done hid_ready hid_used ef_ready summed added hot_ready edges_done n1_done n_silu n2_done "
            "updated step gates")
        gathered = pool_dma_sems(nc, ctx, "gathered0 gathered1 gathered2 gathered3")
        chunk_in = (chunk0, chunk1)
        block = ctx.enter_context(nc.Block())
        NC = len(CHUNKS)

        def before(i, u, lag):
            return (i, u - lag) if u >= lag else (i - 1, u - lag + GROUP)

        def pipeline(eng, steps):
            for u in range(GROUP):
                for lag, f in enumerate(steps):
                    if u >= lag:
                        f(0, u - lag)
            eng.sem_inc(gates, 1)
            with eng.Fori(1, TURNS) as i:
                for u in range(GROUP):
                    for lag, f in enumerate(steps):
                        f(*before(i, u, lag))
            for u in range(GROUP, GROUP + len(steps) - 1):
                for lag, f in enumerate(steps):
                    if u - lag < GROUP:
                        f(TURNS - 1, u - lag)

        @block.sync
        def _(sp):
            with sp.Fori(0, LAYERS) as l:
                sp.wait_ge(layer_done, l + 1)
                one = bass.ds(l, 1)
                w1, nw1 = w["L3_gnn_edge_w1"], w["L3_gnn_node_w1"]
                for k in range(2):
                    sp.dma_start(w_ab[:, k, :], w1[one, k * HID:(k + 1) * HID, :].rearrange("o k h -> (o k) h")).then_inc(w_in, 16)
                for r in range(9):
                    sp.dma_start(w_c[r * EA:(r + 1) * EA, :],
                                 w1[one, 2 * HID:2 * HID + EA, :].rearrange("o k h -> (o k) h")).then_inc(w_in, 16)
                for r in range(3):
                    sp.dma_start(m.b2_rows[r:r + 1, :], w["L3_gnn_edge_b2"][one, :]).then_inc(w_in, 16)
                sp.dma_start(w_2[:, :], w["L3_gnn_edge_w2"][one, :, :].rearrange("o k h -> (o k) h")).then_inc(w_in, 16)
                sp.dma_start(n_1[:, :, :], nw1[one, :, :].rearrange("o (a k) h -> k (o a) h", a=2)).then_inc(w_in, 16)
                sp.dma_start(n_2[:, :], w["L3_gnn_node_w2"][one, :, :].rearrange("o k h -> (o k) h")).then_inc(w_in, 16)
                sp.dma_start(biases[:, 0:1], w["L3_gnn_edge_b1"][one, :].rearrange("o h -> h o")).then_inc(w_in, 16)
                sp.dma_start(biases[:, 1:2], w["L3_gnn_node_b1"][one, :].rearrange("o h -> h o")).then_inc(w_in, 16)
                sp.dma_start(biases[:, 2:3], w["L3_gnn_node_b2"][one, :].rearrange("o h -> h o")).then_inc(w_in, 16)
                sp.wait_ge(q_kept, l * BLOCKS + (BLOCKS + 2))
                sp.dma_start(m.tab3.rearrange("(b p) f -> p b f", p=BN), q_sb[:, :, :]).then_inc(q_out, 16)
                with sp.Fori(0, TURNS) as i:
                    for h in range(2):
                        sp.wait_ge(z_done, l * TILES + i * GROUP + (2 * h + 2))
                        cols = slice(h * 2 * TILE, (h + 1) * 2 * TILE)
                        sp.dma_start(ohT[:, cols], m.ohT[bass.ds(i, 1), :, cols].rearrange("o p c -> (o p) c"))\
                            .then_inc(chunk_in[h], 16)
                        sp.dma_start(atT[:, cols], m.atT[bass.ds(i, 1), :, cols].rearrange("o p c -> (o p) c"))\
                            .then_inc(chunk_in[h], 16)

        @block.gpsimd
        def _(gp):
            with gp.Fori(0, LAYERS) as l:
                gp.wait_ge(q_out, l * 16 + 16)
                gp.sem_inc(m.pool_steps, 1)
                with gp.Fori(0, TURNS) as i:
                    for h in range(2):
                        gather_half(nc, gp, m, i, h, idx, q_got, m.tab3, gathered, (z_done,), idx_ready,
                                    l * TILES, l * (2 * TURNS))

        @block.tensor
        def _(pe):
            pe.sem_inc(z_done, GROUP)
            pe.sem_inc(hid_used, 2)
            pe.sem_inc(summed, 2)
            with pe.Fori(0, LAYERS) as l:
                pe.wait_ge(w_in, l * (16 * W_DMAS) + 16 * W_DMAS)
                pe.wait_ge(updated, l * NC + NC)
                for b in range(BLOCKS):
                    pe.wait_ge(q_kept, l * BLOCKS + (b + 1))
                    nc.tensor.matmul(psY[b % 2][0:BN, 0:HID], m.h[:, b * BN:(b + 1) * BN], w_ab[:, 1, :],
                                     start=True, stop=True).then_inc(q_projected, 1)
                for b in range(BLOCKS):
                    pe.wait_ge(kept, l * BLOCKS + (b + 1))
                    nc.tensor.matmul(psZ[b % 2][0:BN, 0:HID], m.h[:, b * BN:(b + 1) * BN], w_ab[:, 0, :],
                                     start=True, stop=True).then_inc(projected, 1)
                pe.wait_ge(kept, l * BLOCKS + (BLOCKS + 2))
                pe.wait_ge(q_kept, l * BLOCKS + (BLOCKS + 2))
                pe.wait_ge(w_split, l + 1)
                pe.sem_inc(gates, 1)

                def hidden(i, u):
                    t = l * TILES + i * GROUP
                    blk = block_of(pe, m, i, u)
                    pe.wait_ge(hid_ready, t + (u + 1))
                    cols = slice(u * TILE, (u + 1) * TILE)
                    if u % 2 == 0:
                        pe.wait_ge(chunk_in[u // 2], l * (32 * TURNS) + (i * 32 + 32))
                    out = psZ[u % 2][:, 0:TILE]
                    nc.tensor.matmul(out, wc_parts[:, :], atT[:, cols], start=True, stop=False, skip_group_check=True)
                    for k in range(3):
                        nc.tensor.matmul(out, flat(rows[:, bass.ds(blk, 1), k, :]), ohT[:, cols], start=False, stop=False,
                                         skip_group_check=True)
                    pe.wait_ge(gathered[u], l * (32 * TURNS) + (i * 32 + 32))
                    for s in range(SUBS):
                        last = nc.tensor.matmul(psZ[u % 2][:, s * P:(s + 1) * P], q_got[:, u * SUBS + s, :], m.ident[:, :],
                                                start=False, stop=(s == SUBS - 1), is_transpose=True, skip_group_check=True)
                    last.then_inc(z_done, 1)

                def features(i, u):
                    t = l * TILES + i * GROUP
                    pe.wait_ge(ef_ready, t + (u + 1))
                    pe.wait_ge(hid_ready, t + (u + 1 + 2))
                    for s in range(SUBS):
                        out = psY[u % 2][:, s * HID:(s + 1) * HID]
                        nc.tensor.matmul(out, m.ones3[:, :], m.b2_parts[:, :], start=True, stop=False)
                        last = nc.tensor.matmul(out, hid[:, u % 2, s * P:(s + 1) * P], w_2[:, :], start=False, stop=True)
                    last.then_inc(hid_used, 1)

                def sums(i, u):
                    t = l * TILES + i * GROUP
                    pe.wait_ge(added, t + (u + 1))
                    pe.wait_ge(hot_ready, t + (u + 1))
                    pe.wait_ge(ef_ready, t + (u + 1 + 2))
                    for s in range(SUBS):
                        last = nc.tensor.matmul(psS[u % 2][:, 0:BN], ef[:, u % 2, s, :], oh[:, (u % 2) * SUBS + s, :],
                                                start=(s == 0), stop=(s == SUBS - 1))
                    last.then_inc(summed, 1)

                pipeline(pe, (hidden, features, sums))
                pe.wait_ge(edges_done, l + 1)
                for k, (c, n) in enumerate(CHUNKS):
                    pe.wait_ge(n_silu, l * NC + (k + 1))
                    for a, v in enumerate((m.h, agg)):
                        last = nc.tensor.matmul(psZ[k % 2][:, 0:n], n_1[:, a, :], v[:, c:c + n], start=(a == 0), stop=(a == 1))
                    last.then_inc(n1_done, 1)
                    pe.wait_ge(n_silu, l * NC + (k + 1 + 2))
                    if k >= 2:
                        pe.wait_ge(updated, l * NC + (NC + k - 1))
                    nc.tensor.matmul(psY[k % 2][:, 0:n], n_2[:, :], n_hid[:, k % 2, 0:n], start=True, stop=True)\
                        .then_inc(n2_done, 1)

        @block.scalar
        def _(act):
            act.sem_inc(hid_ready, 2)
            act.sem_inc(ef_ready, 2)
            act.sem_inc(n_silu, 2)
            act.sem_inc(q_kept, 2)
            with act.Fori(0, LAYERS) as l:
                for b in range(BLOCKS):
                    act.wait_ge(q_projected, l * BLOCKS + (b + 1))
                    if b == 0:
                        act.wait_ge(layer_done, l + 1)
                    nc.scalar.copy(q_sb[:, b, :], psY[b % 2][0:BN, 0:HID]).then_inc(q_kept, 1)

                def hidden(i, u):
                    t = l * TILES + i * GROUP
                    act.wait_ge(z_done, t + (u + 1 + GROUP))
                    act.wait_ge(hid_used, t + (u + 1))
                    nc.scalar.activation(hid[:, u % 2, :], psZ[u % 2][:, 0:TILE], ACT.Silu, bias=biases[:, 0:1])\
                        .then_inc(hid_ready, 1)

                def features(i, u):
                    t = l * TILES + i * GROUP
                    act.wait_ge(hid_used, t + (u + 1 + 2))
                    act.wait_ge(summed, t + (u + 1))
                    nc.scalar.activation(ef[:, u % 2, :, :].rearrange("p s h -> p (s h)"), psY[u % 2][:, 0:SUBS * HID],
                                         ACT.Silu).then_inc(ef_ready, 1)

                pipeline(act, (hidden, features))
                for k, (c, n) in enumerate(CHUNKS):
                    act.wait_ge(n1_done, l * NC + (k + 1))
                    if k >= 2:
                        act.wait_ge(n2_done, l * NC + (k - 1))
                    nc.scalar.activation(n_hid[:, k % 2, 0:n], psZ[k % 2][:, 0:n], ACT.Silu, bias=biases[:, 1:2])\
                        .then_inc(n_silu, 1)

        @block.vector
        def _(dve):
            dve.sem_inc(added, 2)
            dve.sem_inc(kept, 2)
            dve.sem_inc(updated, NC)
            dve.sem_inc(layer_done, 1)
            LAYER_STEPS = 14 + 4 * BLOCKS + NC + TURNS
            with dve.Fori(0, LAYERS) as l:
                link = Links(dve, step)
                link.base = l * LAYER_STEPS
                dve.wait_ge(w_in, l * (16 * W_DMAS) + 16 * W_DMAS)
                split_rows(nc, link, wc_parts[:, :], w_c[:, :], m.row_masks[:, :], *(wc_tmp[:, k, :] for k in range(3)), w_c[:, :])
                split_rows(nc, link, m.b2_parts[:, :], m.b2_rows[:, :], m.ident[0:3, 0:3],
                           *(m.b2_tmp[:, k, :] for k in range(3)), m.b2_rows[:, :])
                dve.sem_inc(w_split, 1)
                for b in range(BLOCKS):
                    dve.wait_ge(projected, l * BLOCKS + (b + 1))
                    split3(nc, link, tuple(rows[:, b, k, :] for k in range(3)), psZ[b % 2][0:BN, 0:HID], rest[:, :])
                    dve.sem_inc(kept, 1)
                nc.vector.memset(agg[:, :], 0.0)

                def build(i, u):
                    t = l * TILES + i * GROUP
                    if u == 0:
                        ins = nc.vector.tensor_copy(rec[:, :, :], m.meta[:, i * NS:(i + 1) * NS, :] if isinstance(i, int)
                                                    else m.meta[:, bass.ds(i * NS, NS), :])
                        ins.then_inc(step, 1)
                        dve.wait_ge(step, l * LAYER_STEPS + (14 + 4 * BLOCKS) + (i + 1))
                    dve.wait_ge(summed, t + (u + 1))
                    for s in range(SUBS):
                        r = rec[:, u * SUBS + s, :]
                        last = nc.vector.tensor_scalar(oh[:, (u % 2) * SUBS + s, :], m.iota[:, 0:BN], r[:, W_REL:W_REL + 1],
                                                       r[:, W_EW:W_EW + 1], ALU.is_equal, ALU.mult)
                    last.then_inc(hot_ready, 1)

                def add(i, u):
                    t = l * TILES + i * GROUP
                    blk = block_of(dve, m, i, u)
                    dve.wait_ge(summed, t + (u + 1 + 2))
                    to = agg[:, bass.ds(blk * BN, BN)]
                    nc.vector.tensor_tensor(to, to, psS[u % 2][:, 0:BN], ALU.add).then_inc(added, 1)
                    dve.wait_ge(added, t + (u + 1 + 2))

                pipeline(dve, (build, add))
                dve.sem_inc(edges_done, 1)
                link.base = l * LAYER_STEPS + (14 + 4 * BLOCKS) + TURNS
                link.n = 0
                for k, (c, n) in enumerate(CHUNKS):
                    dve.wait_ge(n2_done, l * NC + (k + 1))
                    h = m.h[:, c:c + n]
                    link(nc.vector.scalar_tensor_tensor(h, psY[k % 2][:, 0:n], biases[:, 2:3], h, ALU.add, ALU.add))
                    nc.vector.tensor_tensor(h, h, m.node_mask[:, c:c + n], ALU.mult).then_inc(updated, 1)
                dve.wait_ge(updated, l * NC + 2 * NC)
                dve.sem_inc(layer_done, 1)


def read_out(nc, m, w, out):
    with Stage("read_out") as ctx:
        wt = sb(nc, ctx, "weight", [HID, F])
        bt = sb(nc, ctx, "bias", [BN, F])
        mask = sb(nc, ctx, "mask", [BN, BLOCKS])
        o = sb(nc, ctx, "out", [BN, BLOCKS, F])
        sq = sb(nc, ctx, "squares", [BN, BLOCKS, F])
        st = sb(nc, ctx, "row_stats", [BN, 3, BLOCKS])
        ps = bank(nc, ctx, "psum")
        w_in, projected, var_ready, root_ready, step, done, out_done = sems(
            nc, ctx, "w_in projected var_ready root_ready step norm_done out_done")
        block = ctx.enter_context(nc.Block())

        @block.sync
        def _(sp):
            sp.dma_start(wt[:, :], w["L3_gnn_out_w"]).then_inc(w_in, 16)
            sp.dma_start(bt[:, :], w["L3_gnn_out_b"].rearrange("(o f) -> o f", o=1).to_broadcast([BN, F])).then_inc(w_in, 16)
            with nc.allow_non_contiguous_dma(reason="the node mask, node by node, once"):
                sp.dma_start(mask[:, :], w["node_vec1"].rearrange("(b p) o -> p (b o)", p=BN)).then_inc(w_in, 16)
            sp.wait_ge(done, 1)
            sp.dma_start(out.rearrange("(b p) f -> p b f", p=BN), m.x[:, :, :]).then_inc(out_done, 16)
            sp.wait_ge(out_done, 16)

        @block.tensor
        def _(pe):
            pe.wait_ge(w_in, 48)
            for b in range(BLOCKS):
                last = nc.tensor.matmul(ps[0:BN, b * F:(b + 1) * F], m.h[:, b * BN:(b + 1) * BN], wt[:, :], start=True, stop=True)
            last.then_inc(projected, 1)

        @block.vector
        def _(dve):
            link = Links(dve, step)
            full = [BN, BLOCKS, F]
            dve.wait_ge(projected, 1)
            dve.wait_ge(w_in, 48)
            link(nc.vector.tensor_tensor(o[:, :, :], ps[0:BN, 0:BLOCKS * F].rearrange("p (b f) -> p b f", b=BLOCKS),
                                         bt[:, :].unsqueeze(1).to_broadcast(full), ALU.add))
            link(nc.vector.tensor_tensor(o[:, :, :], o[:, :, :], mask[:, :].unsqueeze(2).to_broadcast(full), ALU.mult))
            link(nc.vector.tensor_tensor(m.x[:, :, :], m.x[:, :, :], o[:, :, :], ALU.add))
            norm_steps(nc, dve, link, m, m.x[:, :, :], sq[:, :, :], st, var_ready, root_ready)
            dve.sem_inc(done, 1)

        @block.scalar
        def _(act):
            root(nc, act, st[:, 2, :], var_ready, root_ready)


def program(nc, t, out):
    m = Mem()
    with Stage("kept") as ctx:
        m.ident = sb(nc, ctx, "ident", [P, P])
        m.row_masks = sb(nc, ctx, "row_masks", [AP9, 3])
        m.iota_i = sb(nc, ctx, "iota_int", [P, P], I32)
        m.iota_t = sb(nc, ctx, "iota_tiles", [1, TILES], I32)
        m.iota = sb(nc, ctx, "iota", [P, P])
        m.tile_block = sb(nc, ctx, "tile_block", [1, TILES], I32)
        m.ones3 = sb(nc, ctx, "ones3", [3, P], BF16)
        m.meta = sb(nc, ctx, "slot_records", [P, NSUB, PW])
        m.x = sb(nc, ctx, "x_nodes", [BN, BLOCKS, F])
        m.acc = sb(nc, ctx, "sums_by_src", [BN, BLOCKS, F + 1])
        m.deg_dst = sb(nc, ctx, "degree_dst", [BN, BLOCKS])
        m.x_in = ctx.enter_context(nc.semaphore("x_in"))
        m.rows1 = sb(nc, ctx, "rows_of_src_parts", [BN, BLOCKS, 3, T1W], BF16)
        m.w2_pair = sb(nc, ctx, "w2_pair", [2 * R1, 2 * F])
        m.b2_rows = sb(nc, ctx, "b2_rows", [3, P])
        m.b2_tmp = sb(nc, ctx, "b2_parts_whole", [3, 3, P], BF16)
        m.b2_parts = sb(nc, ctx, "b2_parts", [3, P], BF16)
        m.conv = sb(nc, ctx, "conv_out", [BN, BLOCKS, F])
        m.scaled = sb(nc, ctx, "conv_scaled", [BN, BLOCKS, F])
        m.rows2 = sb(nc, ctx, "conv_scaled_parts", [BN, BLOCKS, 3, F], BF16)
        m.dinv = sb(nc, ctx, "root_degree", [BN, BLOCKS])
        m.h = sb(nc, ctx, "h", [HID, N])
        m.node_mask = sb(nc, ctx, "node_mask", [HID, N])
        m.tab3 = nc.dram_tensor("egnn_table_of_dst", (N, HID), F32).ap()
        m.tab1 = nc.dram_tensor("sheaf_table_of_dst", (N, T1W), F32).ap()
        m.pool_steps = ctx.enter_context(nc.semaphore("pool_steps"))
        m.slots = nc.dram_tensor("slot_table", (P * ROWC, PW), F32).ap()
        m.ytab = nc.dram_tensor("y_table", (N, F + 1), F32).ap()
        m.ohT = nc.dram_tensor("one_hot_src_T", (TURNS, BN, GROUP * TILE), BF16).ap()
        m.atT = nc.dram_tensor("attr_parts_T", (TURNS, AP9, GROUP * TILE), BF16).ap()
        sort_edges(nc, m, t["src"], t["dst"], t["edge_attr_4"], t["edge_weight1"])
        first_pass(nc, m, t["x"], t["dst"])
        nodes_before_l1(nc, m, t)
        sheaf_edges(nc, m)
        residual_norm(nc, m, "after_l1", m.acc, relu=True)
        conv_nodes_in(nc, m, "conv1_nodes", t["L2_gnn_W1"], m.x)
        conv_edges(nc, m, "conv1_edges", t["L2_gnn_b1"], m.conv, False)
        conv_nodes_in(nc, m, "conv2_nodes", t["L2_gnn_W2"], m.conv)
        conv_edges(nc, m, "conv2_edges", t["L2_gnn_b2"], m.conv, True)
        residual_norm(nc, m, "after_l2", m.conv)
        embed(nc, m, t)
        egnn_layers(nc, m, t)
        read_out(nc, m, t, out)


def kernel(**inputs):
    import concourse.bacc as bacc
    from concourse.bass_utils import run_bass_kernel_spmd as run
    nc = bacc.Bacc("TRN2", target_bir_lowering=False, num_devices=1)
    arrays, t = {}, {}
    for name, a in inputs.items():
        a = np.ascontiguousarray(a)
        arrays["in_" + name] = a
        t[name] = nc.dram_tensor("in_" + name, a.shape, mybir.dt.from_np(a.dtype), kind="ExternalInput").ap()
    out = nc.dram_tensor("out_x", (N, F), F32, kind="ExternalOutput").ap()
    program(nc, t, out)
    return run(nc, [arrays], core_ids=[0]).results[0]["out_x"]
```

```python
import math
from contextlib import ExitStack

import numpy as np
import concourse.bass as bass
from concourse import mybir

F32 = mybir.dt.float32
BF16 = mybir.dt.bfloat16
I32 = mybir.dt.int32
ALU = mybir.AluOpType
ACT = mybir.ActivationFunctionType
AX = mybir.AxisListType.X

P = 128
N = 3125
E = 103125
F = 16
HID = 128
LAYERS = 4
EA = 4
R1 = 64
BN = 125
BLOCKS = N // BN
COLS = -(-E // P)
LASTROW = E - (P - 1) * COLS
SUBS = 2
TILE = SUBS * P
GROUP = 4
NS = GROUP * SUBS
TURNS = -(-((E + BLOCKS * (TILE - 1)) // TILE) // GROUP)
TILES = TURNS * GROUP
NSUB = TILES * SUBS
ROWC = NSUB + 1
PADSRC = 4000
SC_HALF = 13
SC_TURNS = COLS // (2 * SC_HALF)
W_DST, W_REL, W_VALID, W_EW, W_ATTR, W_DLO, W_DHI, PW = 0, 1, 2, 3, 4, 8, 9, 10
AP9 = 9 * EA
T1W = 2 * R1 + F + 1
EPS_LN = 1e-5
assert SC_TURNS * 2 * SC_HALF == COLS and BLOCKS * BN == N and NSUB % NS == 0


class Links:

    def __init__(self, eng, sem):
        self.eng, self.sem, self.n, self.base = eng, sem, 0, 0

    def __call__(self, ins, meanwhile=None):
        self.n += 1
        ins.then_inc(self.sem, 1)
        if meanwhile is not None:
            next(meanwhile, None)
        self.eng.wait_ge(self.sem, self.base + self.n)
        return ins


def split3(nc, link, parts, value, rest):
    link(nc.vector.tensor_copy(parts[0], value))
    link(nc.vector.tensor_tensor(rest, value, parts[0], ALU.subtract))
    link(nc.vector.tensor_copy(parts[1], rest))
    link(nc.vector.tensor_tensor(parts[2], rest, parts[1], ALU.subtract))


def split_rows(nc, link, out, value, row_masks, a, b, c, rest):
    split3(nc, link, (a, b, c), value, rest)
    link(nc.vector.tensor_scalar(out, a, row_masks[:, 0:1], None, ALU.mult))
    link(nc.vector.scalar_tensor_tensor(out, b, row_masks[:, 1:2], out, ALU.mult, ALU.add))
    link(nc.vector.scalar_tensor_tensor(out, c, row_masks[:, 2:3], out, ALU.mult, ALU.add))


def layer_norm(nc, link, out, x, sq, st):
    wide = [BN, BLOCKS, F]
    s, m, v = st[:, 0, :], st[:, 1, :], st[:, 2, :]
    link(nc.vector.tensor_reduce(s, x, AX, ALU.add))
    link(nc.vector.tensor_scalar(m, s, 1.0 / F, None, ALU.mult))
    link(nc.vector.tensor_tensor(out, x, m.unsqueeze(2).to_broadcast(wide), ALU.subtract))
    link(nc.vector.tensor_tensor(sq, out, out, ALU.mult))
    link(nc.vector.tensor_reduce(s, sq, AX, ALU.add))
    link(nc.vector.tensor_scalar(v, s, 1.0 / F, EPS_LN, ALU.mult, ALU.add))
    yield v
    link(nc.vector.reciprocal(m, v))
    link(nc.vector.tensor_tensor(out, out, m.unsqueeze(2).to_broadcast(wide), ALU.mult))


def gather_half(nc, gp, m, i, h, idx, rows, table, gathered, rows_used, idx_ready):
    half = NS // 2
    for used in rows_used:
        gp.wait_ge(used, i * GROUP + (2 * h + 2))
    gp.sem_inc(m.pool_steps, 1)
    nc.gpsimd.tensor_copy(idx[:, h * half:(h + 1) * half],
                          m.meta[:, bass.ds(i * NS + h * half, half), W_DST].bitcast(I32)).then_inc(idx_ready, 1)
    gp.wait_ge(idx_ready, i * 2 + (h + 1))
    gp.sem_inc(m.pool_steps, 1)
    for u in (2 * h, 2 * h + 1):
        for s in range(u * SUBS, (u + 1) * SUBS):
            gp.indirect_dma_start(rows[:, s, :], None, table,
                                  bass.IndirectOffsetOnAxis(ap=idx[:, s:s + 1], axis=0)).then_inc(gathered[u], 16)


def gather_turn(nc, gp, m, i, idx, rows, table, gathered, rows_used, idx_ready, tiles_before=0, turns_before=0):
    gp.wait_ge(rows_used, tiles_before + (i * GROUP + GROUP))
    gp.sem_inc(m.pool_steps, 1)
    nc.gpsimd.tensor_copy(idx[:, :], (m.meta[:, i * NS:(i + 1) * NS, W_DST] if isinstance(i, int) else
                                      m.meta[:, bass.ds(i * NS, NS), W_DST]).bitcast(I32)).then_inc(idx_ready, 1)
    gp.wait_ge(idx_ready, turns_before + (i + 1))
    gp.sem_inc(m.pool_steps, 1)
    for s in range(NS):
        gp.indirect_dma_start(rows[:, s, :], None, table,
                              bass.IndirectOffsetOnAxis(ap=idx[:, s:s + 1], axis=0)).then_inc(gathered[s // SUBS], 16)


def one_hots(nc, m, rec, src=None, dst_low=None, dst_high=None):
    for s in range(SUBS):
        if src is not None:
            last = nc.vector.tensor_scalar(src[:, s, :], m.iota[:, 0:BN], rec[:, s, W_REL:W_REL + 1],
                                           rec[:, s, W_VALID:W_VALID + 1], ALU.is_equal, ALU.mult)
        if dst_low is not None:
            last = nc.vector.tensor_scalar(dst_low[:, s, :], m.iota[:, 0:BN], rec[:, s, W_DLO:W_DLO + 1], None,
                                           ALU.is_equal)
        if dst_high is not None:
            last = nc.vector.tensor_scalar(dst_high[:, s, :], m.iota[:, 0:BLOCKS], rec[:, s, W_DHI:W_DHI + 1],
                                           rec[:, s, W_VALID:W_VALID + 1], ALU.is_equal, ALU.mult)
    return last


def flat(ap):
    return ap.rearrange("p o f -> p (o f)")


def block_of(eng, m, i, u):
    return m.nc.values_load(m.tile_block[0:1, bass.ds(i * GROUP + u, 1)], engines=(eng.engine,), min_val=0,
                            max_val=BLOCKS - 1, skip_runtime_bounds_check_because="sort_edges writes 0 to BLOCKS - 1")


def blocks_of(eng, m, i, regs):
    eng.load(regs, m.tile_block[0:1, bass.ds(i * GROUP, GROUP)])
    return [eng.snap(r, min_val=0, max_val=BLOCKS - 1) for r in regs]


class Mem:
    pass


class Stage(ExitStack):

    def __init__(self, name):
        super().__init__()
        self.name = name


def sb(nc, ctx, name, shape, dt=F32):
    return ctx.enter_context(nc.sbuf_tensor(f"{ctx.name}_{name}", shape, dt))


def bank(nc, ctx, name):
    return ctx.enter_context(nc.psum_tensor(f"{ctx.name}_{name}", [P, 512], F32))


def sems(nc, ctx, names):
    own = [ctx.enter_context(nc.semaphore(f"{ctx.name}_{n}")) for n in names.split()]

    def clear():
        nc.all_engine_barrier()
        for sem in own:
            nc.sync.sem_clear(sem)
        nc.all_engine_barrier()

    ctx.callback(clear)
    return own


def pool_dma_sems(nc, ctx, names):
    return tuple(nc.alloc_semaphore(f"{ctx.name}_{n}") for n in names.split())


def sort_edges(nc, m, src, dst, edge_attr, edge_w):
    NBK = BLOCKS + 1
    with Stage("sort_edges") as ctx:
        raw = sb(nc, ctx, "raw_index", [P, 2, COLS], I32)
        raw_w = sb(nc, ctx, "raw_weight", [P, COLS])
        raw_a = sb(nc, ctx, "raw_attr", [P, COLS * EA])
        srcf = sb(nc, ctx, "src_float", [P, COLS])
        dstf = sb(nc, ctx, "dst_float", [P, COLS])
        above = sb(nc, ctx, "above", [P, COLS])
        mask = sb(nc, ctx, "mask", [P, COLS])
        csum = sb(nc, ctx, "running_count", [P, COLS])
        place = sb(nc, ctx, "place", [P, COLS])
        hi_i = sb(nc, ctx, "place_high", [P, COLS], I32)
        lo_i = sb(nc, ctx, "place_low", [P, COLS], I32)
        row = sb(nc, ctx, "row", [P, COLS], I32)
        rec = sb(nc, ctx, "records", [P, COLS, PW])
        row_buf = sb(nc, ctx, "row_buf", [P, 2, SC_HALF], I32)
        rec_buf = sb(nc, ctx, "record_buf", [P, 2, SC_HALF, PW])
        cnt = sb(nc, ctx, "counts", [P, NBK])
        tri = sb(nc, ctx, "earlier_partition", [P, P])
        ones = sb(nc, ctx, "ones_square", [P, P])
        tot_i = sb(nc, ctx, "block_tiles_int", [P, NBK], I32)
        small = sb(nc, ctx, "small", [P, 6, NBK])
        tidx = sb(nc, ctx, "tile_number", [1, TILES])
        tblk = sb(nc, ctx, "tile_block_float", [1, TILES])
        zrow = sb(nc, ctx, "zero_rows", [P, ROWC])
        ps = bank(nc, ctx, "count_sums")
        (filled, loaded_src, loaded_dst, loaded_w, loaded_attr, const_step, const_ready, zeroed, counted, summed, dve_step,
         placed, copied, meta_in) = sems(
            nc, ctx, "filled loaded_src loaded_dst loaded_w loaded_attr const_step const_ready zeroed counted summed "
            "sort_step placed copied records_loaded")
        scattered = scat0, scat1 = pool_dma_sems(nc, ctx, "scattered0 scattered1")
        block = ctx.enter_context(nc.Block())
        cut = (P - 1) * COLS

        @block.sync
        def _(sp):
            sp.wait_ge(filled, 1)
            for k, (a, sem) in enumerate(((src, loaded_src), (dst, loaded_dst))):
                sp.dma_start(raw[0:P - 1, k, :], a[0:cut].rearrange("(p j) -> p j", p=P - 1)).then_inc(sem, 16)
                sp.dma_start(raw[P - 1:P, k, 0:LASTROW], a[cut:E].rearrange("(p j) -> p j", p=1)).then_inc(sem, 16)
            ew = edge_w.rearrange("e a -> (e a)")
            sp.dma_start(raw_w[0:P - 1, :], ew[0:cut].rearrange("(p j) -> p j", p=P - 1)).then_inc(loaded_w, 16)
            sp.dma_start(raw_w[P - 1:P, 0:LASTROW], ew[cut:E].rearrange("(p j) -> p j", p=1)).then_inc(loaded_w, 16)
            ea = edge_attr.rearrange("e a -> (e a)")
            sp.dma_start(raw_a[0:P - 1, :],
                         ea[0:cut * EA].rearrange("(p j) -> p j", p=P - 1)).then_inc(loaded_attr, 16)
            sp.dma_start(raw_a[P - 1:P, 0:LASTROW * EA],
                         ea[cut * EA:E * EA].rearrange("(p j) -> p j", p=1)).then_inc(loaded_attr, 16)
            zero_src = zrow[:, :]
            for w in range(PW):
                sp.dma_start(m.slots.rearrange("(p c) w -> p (c w)", p=P)[:, w * ROWC:(w + 1) * ROWC],
                             zero_src).then_inc(zeroed, 16)
            sp.wait_ge(scat0, 16 * SC_HALF * SC_TURNS)
            sp.wait_ge(scat1, 16 * SC_HALF * SC_TURNS)
            sp.dma_start(m.meta[:, :, :], m.slots.rearrange("(p c) w -> p c w", p=P)[:, 0:NSUB, :]).then_inc(meta_in, 16)
            sp.wait_ge(meta_in, 16)

        @block.gpsimd
        def _(gp):
            nc.gpsimd.memset(ones[:, :], 1.0).then_inc(const_step, 1)
            nc.gpsimd.memset(m.ident[:, :], 0.0).then_inc(const_step, 1)
            nc.gpsimd.memset(m.row_masks[:, :], 1.0).then_inc(const_step, 1)
            nc.gpsimd.iota(m.iota_i[:, :], [[1, P]], base=0, channel_multiplier=0).then_inc(const_step, 1)
            nc.gpsimd.iota(m.iota_t[:, :], [[1, TILES]], base=0, channel_multiplier=0).then_inc(const_step, 1)
            gp.wait_ge(const_step, 5)
            nc.gpsimd.affine_select(out=tri[:, :], in_=ones[:, :], compare_op=ALU.is_gt, fill=0.0, base=0,
                                    pattern=[[1, P]], channel_multiplier=-1).then_inc(const_ready, 1)
            nc.gpsimd.affine_select(out=m.ident[:, :], in_=m.ident[:, :], compare_op=ALU.not_equal, fill=1.0,
                                    base=0, pattern=[[-1, P]], channel_multiplier=1).then_inc(const_ready, 1)
            nc.gpsimd.affine_select(out=m.row_masks[:, :], in_=m.row_masks[:, :], compare_op=ALU.is_ge, fill=0.0,
                                    base=0, pattern=[[-3 * EA, 3]], channel_multiplier=1).then_inc(const_step, 1)
            gp.wait_ge(const_step, 6)
            nc.gpsimd.affine_select(out=m.row_masks[:, :], in_=m.row_masks[:, :], compare_op=ALU.is_ge, fill=0.0,
                                    base=3 * EA - 1, pattern=[[3 * EA, 3]],
                                    channel_multiplier=-1).then_inc(const_ready, 1)
            gp.wait_ge(zeroed, 16 * PW)
            with gp.Fori(0, SC_TURNS) as i:
                for h in range(2):
                    gp.wait_ge(copied, i * 2 + (h + 1))
                    gp.sem_inc(m.pool_steps, 1)
                    for j in range(SC_HALF):
                        gp.indirect_dma_start(m.slots, bass.IndirectOffsetOnAxis(ap=row_buf[:, h, j:j + 1], axis=0),
                                              rec_buf[:, h, j, :], None).then_inc(scattered[h], 16)

        @block.tensor
        def _(pe):
            pe.wait_ge(const_ready, 3)
            pe.wait_ge(counted, 1)
            nc.tensor.matmul(ps[:, 0:NBK], tri[:, :], cnt[:, :], start=True, stop=True)
            nc.tensor.matmul(ps[:, 64:64 + NBK], ones[:, :], cnt[:, :], start=True, stop=True).then_inc(summed, 1)

        @block.scalar
        def _(act):
            act.wait_ge(placed, 1)
            for h in range(2):
                c = h * SC_HALF
                nc.scalar.copy(rec_buf[:, h, :, :], rec[:, c:c + SC_HALF, :])
                nc.scalar.copy(row_buf[:, h, :], row[:, c:c + SC_HALF]).then_inc(copied, 1)
            with act.Fori(1, SC_TURNS) as i:
                for h in range(2):
                    act.wait_ge(scattered[h], i * (16 * SC_HALF))
                    c = i * (2 * SC_HALF) + h * SC_HALF
                    nc.scalar.copy(rec_buf[:, h, :, :], rec[:, bass.ds(c, SC_HALF), :])
                    nc.scalar.copy(row_buf[:, h, :], row[:, bass.ds(c, SC_HALF)]).then_inc(copied, 1)

        @block.vector
        def _(dve):
            link = Links(dve, dve_step)
            link(nc.vector.memset(raw[:, 0, :], PADSRC))
            link(nc.vector.memset(raw[:, 1, :], 0))
            link(nc.vector.memset(raw_w[:, :], 0.0))
            link(nc.vector.memset(raw_a[:, :], 0.0))
            nc.vector.memset(zrow[:, :], 0.0).then_inc(filled, 1)
            dve.wait_ge(loaded_src, 32)
            link(nc.vector.tensor_copy(srcf[:, :], raw[:, 0, :]))
            link(nc.vector.memset(place[:, :], 0.0))
            for b in range(NBK):
                link(nc.vector.tensor_scalar(above[:, :], srcf[:, :], float(BN * (b + 1)), None, ALU.is_ge))
                if b < BLOCKS:
                    link(nc.vector.scalar_tensor_tensor(mask[:, :], srcf[:, :], float(BN * b), above[:, :],
                                                        ALU.is_ge, ALU.subtract))
                else:
                    link(nc.vector.tensor_scalar(mask[:, :], srcf[:, :], float(BN * b), None, ALU.is_ge))
                link(nc.vector.tensor_tensor_scan(csum[:, :], mask[:, :], mask[:, :], 0.0, ALU.add, ALU.max))
                nc.vector.tensor_copy(cnt[:, b:b + 1], csum[:, COLS - 1:COLS])
                link(nc.vector.tensor_tensor(above[:, :], csum[:, :], mask[:, :], ALU.mult))
                link(nc.vector.tensor_tensor(place[:, :], place[:, :], above[:, :], ALU.add))
            nc.vector.tensor_scalar(place[:, :], place[:, :], -1.0, None, ALU.add).then_inc(counted, 1)
            dve.wait_ge(summed, 1)
            dve.wait_ge(const_ready, 3)
            tiles, start, base, step = (small[:, k, :] for k in range(4))
            link(nc.vector.tensor_scalar(tot_i[:, :], ps[:, 64:64 + NBK], float(TILE - 1), None, ALU.add))
            link(nc.vector.tensor_scalar(tot_i[:, :], tot_i[:, :], int(math.log2(TILE)), None,
                                         ALU.logical_shift_right))
            link(nc.vector.tensor_copy(tiles, tot_i[:, :]))
            link(nc.vector.memset(base, 0.0))
            link(nc.vector.tensor_tensor_scan(start, tiles, base, 0.0, ALU.add, ALU.add))
            link(nc.vector.tensor_tensor(start, start, tiles, ALU.subtract))
            link(nc.vector.memset(start[:, BLOCKS:NBK], float(TILES)))
            link(nc.vector.scalar_tensor_tensor(base, start, float(TILE), ps[:, 0:NBK], ALU.mult, ALU.add))
            link(nc.vector.tensor_copy(step[:, 0:1], base[:, 0:1]))
            link(nc.vector.tensor_tensor(step[:, 1:NBK], base[:, 1:NBK], base[:, 0:NBK - 1], ALU.subtract))
            link(nc.vector.tensor_scalar(place[:, :], place[:, :], step[:, 0:1], None, ALU.add))
            for b in range(1, NBK):
                link(nc.vector.tensor_scalar(above[:, :], srcf[:, :], float(BN * b), step[:, b:b + 1],
                                             ALU.is_ge, ALU.mult))
                link(nc.vector.tensor_tensor(place[:, :], place[:, :], above[:, :], ALU.add))
            link(nc.vector.tensor_copy(row[:, :], place[:, :]))
            link(nc.vector.tensor_scalar(hi_i[:, :], row[:, :], int(math.log2(P)), None, ALU.logical_shift_right))
            link(nc.vector.tensor_scalar(lo_i[:, :], row[:, :], P - 1, None, ALU.bitwise_and))
            link(nc.vector.scalar_tensor_tensor(row[:, :], lo_i[:, :], float(ROWC), hi_i[:, :], ALU.mult, ALU.add))
            for a, (w_lo, w_hi, idx, sem) in enumerate(((W_REL, None, 0, None), (W_DLO, W_DHI, 1, loaded_dst))):
                f = srcf if a == 0 else dstf
                if a == 1:
                    dve.wait_ge(loaded_dst, 32)
                    link(nc.vector.tensor_copy(dstf[:, :], raw[:, 1, :]))
                link(nc.vector.tensor_scalar(mask[:, :], f[:, :], float(BN), None, ALU.is_ge))
                for b in range(2, BLOCKS):
                    link(nc.vector.scalar_tensor_tensor(mask[:, :], f[:, :], float(BN * b), mask[:, :],
                                                        ALU.is_ge, ALU.add))
                link(nc.vector.scalar_tensor_tensor(rec[:, :, w_lo], mask[:, :], -float(BN), f[:, :],
                                                    ALU.mult, ALU.add))
                if w_hi is not None:
                    link(nc.vector.tensor_copy(rec[:, :, w_hi], mask[:, :]))
            link(nc.vector.tensor_copy(rec[:, :, W_DST].bitcast(I32), raw[:, 1, :]))
            link(nc.vector.tensor_scalar(rec[:, :, W_VALID], srcf[:, :], float(N), None, ALU.is_lt))
            dve.wait_ge(loaded_w, 32)
            link(nc.vector.tensor_copy(rec[:, :, W_EW], raw_w[:, :]))
            dve.wait_ge(loaded_attr, 32)
            nc.vector.tensor_copy(rec[:, :, W_ATTR:W_ATTR + EA],
                                  raw_a[:, :].rearrange("p (j a) -> p j a", a=EA)).then_inc(placed, 1)
            link(nc.vector.tensor_copy(m.iota[:, :], m.iota_i[:, :]))
            link(nc.vector.tensor_copy(tidx[:, :], m.iota_t[:, :]))
            link(nc.vector.tensor_scalar(tblk[:, :], tidx[:, :], start[0:1, 1:2], None, ALU.is_ge))
            for b in range(2, BLOCKS):
                link(nc.vector.scalar_tensor_tensor(tblk[:, :], tidx[:, :], start[0:1, b:b + 1], tblk[:, :],
                                                    ALU.is_ge, ALU.add))
            link(nc.vector.tensor_copy(m.tile_block[:, :], tblk[:, :]))
            link(nc.vector.memset(m.ones3[:, :], 1.0))


def first_pass(nc, m, x, dst):
    with Stage("first_pass") as ctx:
        yidx = sb(nc, ctx, "y_index", [BN, BLOCKS], I32)
        ynode = sb(nc, ctx, "y_node", [BN, BLOCKS, F + 1])
        idx = [sb(nc, ctx, f"index_buf{b}", [P, NS], I32) for b in range(2)]
        yg = [sb(nc, ctx, f"y_gathered{b}", [P, NS, F + 1]) for b in range(2)]
        rec = sb(nc, ctx, "turn_records", [P, NS, PW])
        parts = sb(nc, ctx, "attr_parts", [P, NS, 3, 3, EA])
        a_hi = sb(nc, ctx, "attr_hi", [P, NS, EA], BF16)
        a_mid = sb(nc, ctx, "attr_mid", [P, NS, EA], BF16)
        a_lo = sb(nc, ctx, "attr_lo", [P, NS, EA], BF16)
        a_rest = sb(nc, ctx, "attr_rest", [P, NS, EA])
        oh = sb(nc, ctx, "one_hot_src", [P, NS, BN])
        dlo = sb(nc, ctx, "one_hot_dst_low", [P, NS, BN], BF16)
        dhi = sb(nc, ctx, "one_hot_dst_high", [P, NS, BLOCKS], BF16)
        ohT_sb = sb(nc, ctx, "one_hot_srcT", [BN, GROUP * TILE], BF16)
        atT_sb = sb(nc, ctx, "attr_partsT", [AP9, GROUP * TILE], BF16)
        zero = sb(nc, ctx, "zeros", [P, BLOCKS * (F + 1)], BF16)
        psT = [bank(nc, ctx, f"one_hot_T_psum{k}") for k in range(2)]
        psA = [bank(nc, ctx, f"attr_T_psum{k}") for k in range(2)]
        psY = bank(nc, ctx, "sum_psum")
        psD = bank(nc, ctx, "degree_psum")
        (yidx_in, y_out, idx_ready, tile_ready, attr_ready, transposed, copied,
         summed, stored0, stored1, half_free, dve_step, ones_set, deg_done) = sems(
            nc, ctx, "yidx_in y_out idx_ready tile_ready attr_ready transposed "
            "copiedT summed stored0 stored1 half_free pass_step ones_set deg_done")
        y_in, = pool_dma_sems(nc, ctx, "y_in")
        gathered = (pool_dma_sems(nc, ctx, "gathered00 gathered01 gathered02 gathered03"),
                    pool_dma_sems(nc, ctx, "gathered10 gathered11 gathered12 gathered13"))
        stored = (stored0, stored1)
        block = ctx.enter_context(nc.Block())

        @block.sync
        def _(sp):
            sp.dma_start(yidx[:, :], dst[0:N].rearrange("(p b) -> p b", p=BN)).then_inc(yidx_in, 16)
            sp.dma_start(m.x[:, :, :], x.rearrange("(b p) f -> p b f", p=BN)).then_inc(m.x_in, 16)
            sp.wait_ge(y_in, 16 * BLOCKS)
            sp.wait_ge(ones_set, 1)
            sp.dma_start(m.ytab.rearrange("(p b) f -> p b f", p=BN), ynode[:, :, :]).then_inc(y_out, 16)
            sp.sem_inc(half_free, 2)
            with sp.Fori(0, TURNS) as i:
                for h in range(2):
                    sp.wait_ge(copied, i * GROUP + (2 * h + 2 + 2))
                    cols = slice(h * 2 * TILE, (h + 1) * 2 * TILE)
                    sp.dma_start(m.ohT[bass.ds(i, 1), :, cols].rearrange("o p c -> (o p) c"),
                                 ohT_sb[:, cols]).then_inc(stored[h], 16)
                    sp.dma_start(m.atT[bass.ds(i, 1), :, cols].rearrange("o p c -> (o p) c"),
                                 atT_sb[:, cols]).then_inc(stored[h], 16)
                    if h == 1:
                        sp.wait_ge(stored[0], i * 32 + 32)
                        sp.sem_inc(half_free, 1)
                sp.wait_ge(stored[1], i * 32 + 32)
                sp.sem_inc(half_free, 1)

        @block.gpsimd
        def _(gp):
            gp.wait_ge(yidx_in, 16)
            gp.wait_ge(ones_set, 1)
            for b in range(BLOCKS):
                gp.indirect_dma_start(ynode[:, b, 0:F], None, x,
                                      bass.IndirectOffsetOnAxis(ap=yidx[:, b:b + 1], axis=0)).then_inc(y_in, 16)
            gp.wait_ge(y_out, 16)

            def turn(i, b):
                gather_turn(nc, gp, m, i, idx[b], yg[b], m.ytab, gathered[b], summed, idx_ready)

            turn(0, 0)
            with gp.Fori(0, TURNS // 2) as k:
                turn(k * 2 + 1, 1)
                turn(k * 2 + 2, 0)

        @block.vector
        def _(dve):
            link = Links(dve, dve_step)
            nc.vector.memset(ynode[:, :, F:F + 1], 1.0).then_inc(ones_set, 1)
            link(nc.vector.memset(zero[:, :], 0.0))
            PER, first = 5, link.n

            def records(i):
                link.base, link.n = i * PER + first, 0
                if not isinstance(i, int):
                    dve.wait_ge(tile_ready, i * GROUP)
                    dve.wait_ge(attr_ready, i * 1)
                link(nc.vector.tensor_copy(rec[:, :, :], m.meta[:, i * NS:(i + 1) * NS, :] if isinstance(i, int)
                                           else m.meta[:, bass.ds(i * NS, NS), :]))
                split3(nc, link, (a_hi[:, :, :], a_mid[:, :, :], a_lo[:, :, :]), rec[:, :, W_ATTR:W_ATTR + EA],
                       a_rest[:, :, :])
                dve.wait_ge(transposed, i * GROUP + 1)
                for k, part in enumerate((a_hi, a_mid, a_lo)):
                    last = nc.vector.tensor_copy(parts[:, :, :, k, :],
                                                 part[:, :, :].unsqueeze(2).to_broadcast([P, NS, 3, EA]))
                last.then_inc(attr_ready, 1)
                assert link.n == PER

            def build(i, u):
                dve.wait_ge(summed, i * GROUP + (u + 1 + GROUP))
                tile = slice(u * SUBS, (u + 1) * SUBS)
                one_hots(nc, m, rec[:, tile, :], oh[:, tile, :], dlo[:, tile, :], dhi[:, tile, :]).then_inc(tile_ready, 1)

            def turn(i):
                records(i)
                for u in range(GROUP):
                    build(i, u)

            turn(0)
            with dve.Fori(1, TURNS) as i:
                turn(i)
            link.base, link.n = first + PER * TURNS, 0
            dve.wait_ge(deg_done, 1)
            link(nc.vector.tensor_copy(m.deg_dst[:, :], psD[0:BN, 0:BLOCKS]))
            link(nc.vector.tensor_copy(m.acc[:, :, :],
                                       psY[0:BN, 0:BLOCKS * (F + 1)].rearrange("p (b f) -> p b f", b=BLOCKS)))

        @block.tensor
        def _(pe):
            pe.sem_inc(summed, 2 * GROUP)
            pe.sem_inc(transposed, 1)
            pe.wait_ge(dve_step, 1)
            regs = [pe.alloc_register(f"first_pass_block_of_tile{u}") for u in range(GROUP)]
            by_block = psY[0:BN, 0:BLOCKS * (F + 1)].rearrange("p (b f) -> p b f", b=BLOCKS)
            nc.tensor.matmul(psY[0:BN, 0:BLOCKS * (F + 1)], zero[:, 0:BN], zero[:, :], start=True, stop=False,
                             skip_group_check=True)
            nc.tensor.matmul(psD[0:BN, 0:BLOCKS], zero[:, 0:BN], zero[:, 0:BLOCKS], start=True, stop=False,
                             skip_group_check=True)

            def turn(i, b, n):
                blk = blocks_of(pe, m, i, regs)
                pe.wait_ge(attr_ready, i + 1)
                for u in range(GROUP):
                    pe.wait_ge(tile_ready, i * GROUP + (u + 1))
                    pe.wait_ge(copied, i * GROUP + (u + 1))
                    for s in range(SUBS):
                        nc.tensor.transpose(psT[u % 2][0:BN, s * P:(s + 1) * P], oh[:, u * SUBS + s, :], m.ident[:, :])
                    for s in range(SUBS):
                        last = nc.tensor.transpose(psA[u % 2][0:AP9, s * P:(s + 1) * P],
                                                   parts[:, u * SUBS + s, :, :, :].rearrange("p l k a -> p (l k a)"),
                                                   m.ident[:, :])
                    last.then_inc(transposed, 1)
                    for s in range(SUBS):
                        nc.tensor.matmul(psD[0:BN, 0:BLOCKS], dlo[:, u * SUBS + s, :], dhi[:, u * SUBS + s, :],
                                         start=False, stop=False, skip_group_check=True)
                    pe.wait_ge(gathered[b][u], n * 32 + 32)
                    for s in range(SUBS):
                        last = nc.tensor.matmul(flat(by_block[:, bass.ds(blk[u], 1), :]), oh[:, u * SUBS + s, :],
                                                yg[b][:, u * SUBS + s, :], start=False, stop=False, skip_group_check=True)
                    last.then_inc(summed, 1)

            turn(0, 0, 0)
            with pe.Fori(0, TURNS // 2) as k:
                turn(k * 2 + 1, 1, k)
                turn(k * 2 + 2, 0, k + 1)
            nc.tensor.matmul(psY[0:BN, 0:BLOCKS * (F + 1)], zero[:, 0:BN], zero[:, :], start=False, stop=True,
                             skip_group_check=True)
            nc.tensor.matmul(psD[0:BN, 0:BLOCKS], zero[:, 0:BN], zero[:, 0:BLOCKS], start=False, stop=True,
                             skip_group_check=True).then_inc(deg_done, 1)

        @block.scalar
        def _(act):
            act.sem_inc(copied, 2)
            with act.Fori(0, TURNS) as i:
                for u in range(GROUP):
                    if u % 2 == 0:
                        act.wait_ge(half_free, i * 2 + (u // 2 + 1))
                    act.wait_ge(transposed, i * GROUP + (u + 2))
                    nc.scalar.copy(ohT_sb[:, u * TILE:(u + 1) * TILE], psT[u % 2][0:BN, 0:TILE])
                    nc.scalar.copy(atT_sb[:, u * TILE:(u + 1) * TILE], psA[u % 2][0:AP9, 0:TILE]).then_inc(copied, 1)


def norm_steps(nc, dve, link, m, x, sq, st, var_ready, root_ready):
    for _ in layer_norm(nc, link, x, x, sq, st):
        dve.sem_inc(var_ready, 1)
        dve.wait_ge(root_ready, 1)


def root(nc, act, st, var_ready, root_ready):
    act.wait_ge(var_ready, 1)
    nc.scalar.activation(st, st, ACT.Sqrt).then_inc(root_ready, 1)


def transpose_nodes(nc, pe, m, xo, width, banks, xT, transposed, copied):
    for k in range(-(-BLOCKS // 4)):
        if k >= 2:
            pe.wait_ge(copied, k - 1)
        for b in range(4 * k, min(4 * k + 4, BLOCKS)):
            last = nc.tensor.transpose(banks[k % 2][0:width, (b - 4 * k) * BN:(b - 4 * k + 1) * BN], xo[:, b, :],
                                       m.ident[0:BN, 0:BN])
        last.then_inc(transposed, 1)


def copy_transposed(nc, act, width, banks, xT, transposed, copied):
    for k in range(-(-BLOCKS // 4)):
        act.wait_ge(transposed, k + 1)
        n = min(4 * k + 4, BLOCKS) - 4 * k
        nc.scalar.copy(xT[0:width, 4 * k * BN:(4 * k + n) * BN], banks[k % 2][0:width, 0:n * BN]).then_inc(copied, 1)


def nodes_before_l1(nc, m, w):
    with Stage("nodes_before_l1") as ctx:
        sq = sb(nc, ctx, "squares", [BN, BLOCKS, F])
        st = sb(nc, ctx, "row_stats", [BN, 3, BLOCKS])
        deg = sb(nc, ctx, "degree", [BN, BLOCKS])
        xo = sb(nc, ctx, "x_and_one", [BN, BLOCKS, F + 1])
        xT = sb(nc, ctx, "xT", [F + 1, N])
        w1_sb = sb(nc, ctx, "w1_both", [F + 1, 4, R1])
        to_src = sb(nc, ctx, "rows_of_src", [BN, BLOCKS, T1W])
        to_dst = sb(nc, ctx, "rows_of_dst", [BN, BLOCKS, T1W])
        pT = [bank(nc, ctx, f"xT_psum{k}") for k in range(2)]
        pW = [bank(nc, ctx, f"project_psum{k}") for k in range(2)]
        (var_ready, root_ready, step, w_zero, w_in, bd_zero, bd_in, b2_in, x_ready, transposed, copied, projected, drained,
         deg_ready, deg_root, tab_ready, tab_out) = sems(
            nc, ctx, "var_ready root_ready norm_step w_zero w_in bd_zero bd_in b2_in x_ready xT_psum_ready xT_ready "
            "projected drained deg_ready deg_root table_ready table_out")
        block = ctx.enter_context(nc.Block())

        @block.sync
        def _(sp):
            sp.wait_ge(w_zero, 1)
            w1, b1, w2, b2 = w["L1_gnn_W1"], w["L1_gnn_b1"], w["L1_gnn_W2"], w["L1_gnn_b2"]
            with nc.allow_non_contiguous_dma(reason="a small weight, transposed"):
                for k, part in enumerate((0, 1, 1, 0)):
                    sp.dma_start(w1_sb[0:F, k, :], w1[:, part * F:(part + 1) * F].rearrange("h f -> f h")).then_inc(w_in, 16)
                for k in (0, 3):
                    sp.dma_start(w1_sb[F:F + 1, k, :], b1.rearrange("(o h) -> o h", o=1)).then_inc(w_in, 16)
                for k in range(2):
                    sp.dma_start(m.w2_pair[k * R1:(k + 1) * R1, k * F:(k + 1) * F],
                                 w2.rearrange("f h -> h f")).then_inc(bd_in, 16)
            for r in range(3):
                for k in range(2):
                    sp.dma_start(m.b2_rows[r:r + 1, k * F:(k + 1) * F],
                                 b2.rearrange("(o f) -> o f", o=1)).then_inc(b2_in, 16)
            sp.wait_ge(tab_ready, 1)
            sp.dma_start(m.tab1.rearrange("(b p) f -> p b f", p=BN), to_dst[:, :, :]).then_inc(tab_out, 16)
            sp.wait_ge(tab_out, 16)

        @block.gpsimd
        def _(gp):
            nc.gpsimd.memset(w1_sb[:, :, :], 0.0)
            nc.gpsimd.memset(m.w2_pair[:, :], 0.0).then_inc(w_zero, 1)

        @block.vector
        def _(dve):
            link = Links(dve, step)
            dve.wait_ge(m.x_in, 16)
            link(nc.vector.tensor_tensor(m.x[:, :, :], m.x[:, :, :], m.acc[:, :, 0:F], ALU.add))
            norm_steps(nc, dve, link, m, m.x[:, :, :], sq[:, :, :], st, var_ready, root_ready)
            link(nc.vector.memset(xo[:, :, :], 1.0))
            nc.vector.tensor_copy(xo[:, :, 0:F], m.x[:, :, :]).then_inc(x_ready, 1)
            link(nc.vector.tensor_tensor(deg[:, :], m.acc[:, :, F], m.deg_dst[:, :], ALU.add))
            nc.vector.tensor_scalar(deg[:, :], deg[:, :], 1e-5, None, ALU.max).then_inc(deg_ready, 1)
            dve.wait_ge(deg_root, 1)
            dve.wait_ge(x_ready, 1)
            link(nc.vector.reciprocal(deg[:, :], deg[:, :]))
            for t in (to_src, to_dst):
                nc.vector.tensor_copy(t[:, :, 2 * R1:2 * R1 + F], m.x[:, :, :])
                nc.vector.tensor_copy(t[:, :, 2 * R1 + F], deg[:, :])
            for b in range(BLOCKS):
                dve.wait_ge(projected, b + 1)
                nc.vector.tensor_copy(to_src[:, b, 0:2 * R1], pW[b % 2][0:BN, 0:2 * R1])
                ins = nc.vector.tensor_copy(to_dst[:, b, 0:2 * R1], pW[b % 2][0:BN, 2 * R1:4 * R1])
                ins.then_inc(drained, 1)
            dve.wait_ge(drained, BLOCKS)
            dve.sem_inc(tab_ready, 1)
            parts = tuple(m.rows1[:, :, k, :] for k in range(3))
            split3(nc, link, parts, to_src[:, :, :], to_src[:, :, :])
            dve.wait_ge(b2_in, 96)
            split_rows(nc, link, m.b2_parts[:, 0:2 * F], m.b2_rows[:, 0:2 * F], m.ident[0:3, 0:3],
                       *(m.b2_tmp[:, k, 0:2 * F] for k in range(3)), m.b2_rows[:, 0:2 * F])
            dve.wait_ge(bd_in, 32)

        @block.scalar
        def _(act):
            root(nc, act, st[:, 2, :], var_ready, root_ready)
            act.wait_ge(deg_ready, 1)
            nc.scalar.activation(deg[:, :], deg[:, :], ACT.Sqrt).then_inc(deg_root, 1)
            copy_transposed(nc, act, F + 1, pT, xT, transposed, copied)

        @block.tensor
        def _(pe):
            pe.wait_ge(x_ready, 1)
            transpose_nodes(nc, pe, m, xo, F + 1, pT, xT, transposed, copied)
            pe.wait_ge(w_in, 96)
            pe.wait_ge(copied, -(-BLOCKS // 4))
            for b in range(BLOCKS):
                if b >= 2:
                    pe.wait_ge(drained, b - 1)
                nc.tensor.matmul(pW[b % 2][0:BN, 0:4 * R1], xT[:, b * BN:(b + 1) * BN],
                                 w1_sb[:, :, :].rearrange("p k h -> p (k h)"), start=True, stop=True).then_inc(projected, 1)


def sheaf_edges(nc, m):
    PAIR, HALF = [P, NS, 2, F], NS // 2
    with Stage("sheaf_edges") as ctx:
        idx = sb(nc, ctx, "index_buf", [P, NS], I32)
        rows = sb(nc, ctx, "rows_gathered", [P, NS, T1W])
        ohT = sb(nc, ctx, "one_hot_chunk", [BN, GROUP * TILE], BF16)
        rec = sb(nc, ctx, "turn_records", [P, NS, PW])
        hid = sb(nc, ctx, "hidden", [P, 2, TILE])
        xs = sb(nc, ctx, "x_src_dst", [P, NS, 2, F + 1])
        x_dst = sb(nc, ctx, "x_dst", [P, NS, F + 1])
        vu = sb(nc, ctx, "reflectors", [P, NS, 2, F])
        w = sb(nc, ctx, "reflected_once", [P, NS, 2, F])
        msg = sb(nc, ctx, "messages", [P, NS, 2, F])
        msg_src = sb(nc, ctx, "messages_to_src", [P, NS, F])
        prod = sb(nc, ctx, "products", [P, NS, 2, F])
        dots = sb(nc, ctx, "dots", [P, NS, 2])
        rcp = sb(nc, ctx, "two_over_norm", [P, NS, 2])
        coef = sb(nc, ctx, "coefficients", [P, NS])
        low = sb(nc, ctx, "dst_low", [P, NS])
        dist = sb(nc, ctx, "distance", [P, NS, BN])
        oh = sb(nc, ctx, "one_hot_src", [P, NS, BN])
        dlo = sb(nc, ctx, "one_hot_dst_low", [P, NS, BN])
        dhi = sb(nc, ctx, "one_hot_dst_high", [P, NS, BLOCKS])
        wide = sb(nc, ctx, "messages_by_block", [P, NS, BLOCKS, F])
        zero = sb(nc, ctx, "zero_square", [P, BLOCKS * F], BF16)
        psZ = [bank(nc, ctx, f"hidden_psum{k}") for k in range(2)]
        psV = [bank(nc, ctx, f"reflector_psum{h}") for h in range(2)]
        psX = [bank(nc, ctx, f"x_src_psum{h}") for h in range(2)]
        psD = bank(nc, ctx, "node_sum_psum")
        (idx_ready, chunk0, chunk1, z_done, z_ready, hid_ready, hid_used, half_in, turn_in, x_in,
         math_done, math_step, tile_ready, summed, zeroed, d_done, act_step, low_ready) = sems(
            nc, ctx, "idx_ready chunk_in0 chunk_in1 z_done z_ready hid_ready hid_used "
            "half_in turn_in x_dst_in math_done math_step tile_ready summed zeroed d_done act_step low_ready")
        gathered = pool_dma_sems(nc, ctx, "gathered0 gathered1 gathered2 gathered3")
        chunk_in = (chunk0, chunk1)
        block = ctx.enter_context(nc.Block())

        @block.sync
        def _(sp):
            load_chunks(nc, sp, m, ohT, chunk_in, z_done)

        @block.gpsimd
        def _(gp):
            with gp.Fori(0, TURNS) as i:
                for h in range(2):
                    gather_half(nc, gp, m, i, h, idx, rows, m.tab1, gathered, (z_done, x_in), idx_ready)

        @block.tensor
        def _(pe):
            pe.sem_inc(z_done, GROUP)
            pe.sem_inc(hid_used, 2)
            pe.sem_inc(summed, GROUP)
            pe.wait_ge(zeroed, 1)
            regs = [pe.alloc_register(f"sheaf_block_of_tile{u}") for u in range(GROUP)]
            sum_regs = [pe.alloc_register(f"sheaf_block_of_summed_tile{u}") for u in range(GROUP)]
            by_block = psD[0:BN, 0:BLOCKS * F].rearrange("p (b f) -> p b f", b=BLOCKS)
            nc.tensor.matmul(psD[0:BN, 0:BLOCKS * F], zero[:, 0:BN], zero[:, :], start=True, stop=False,
                             skip_group_check=True)

            def hidden(i, u, blk):
                pe.wait_ge(hid_ready, i * GROUP + (u + 1))
                cols = slice(u * TILE, (u + 1) * TILE)
                if u % 2 == 0:
                    pe.wait_ge(chunk_in[u // 2], i * 16 + 16)
                for k in range(3):
                    nc.tensor.matmul(psZ[u % 2][:, 0:TILE], flat(m.rows1[:, bass.ds(blk, 1), k, 0:2 * R1]),
                                     ohT[:, cols], start=(k == 0), stop=False, skip_group_check=True)
                pe.wait_ge(gathered[u], i * 32 + 32)
                for s in range(SUBS):
                    last = nc.tensor.matmul(psZ[u % 2][:, s * P:(s + 1) * P], rows[:, u * SUBS + s, 0:2 * R1],
                                            m.ident[:, :], start=False, stop=(s == SUBS - 1), is_transpose=True,
                                            skip_group_check=True)
                last.then_inc(z_ready, 1)
                for s in range(u * SUBS, (u + 1) * SUBS):
                    for k in range(3):
                        last = nc.tensor.matmul(psX[u // 2][:, s % HALF * (F + 1):(s % HALF + 1) * (F + 1)], ohT[:, s * P:(s + 1) * P],
                                                flat(m.rows1[:, bass.ds(blk, 1), k, 2 * R1:T1W]),
                                                start=(k == 0), stop=(k == 2))
                last.then_inc(z_done, 1)

            def reflectors(i, u):
                pe.wait_ge(hid_ready, i * GROUP + (u + 1 + 2))
                for s in range(SUBS):
                    at = u % 2 * SUBS + s
                    out = psV[u // 2][:, at * 2 * F:(at + 1) * 2 * F]
                    nc.tensor.matmul(out, m.ones3[:, :], m.b2_parts[:, 0:2 * F], start=True, stop=False)
                    last = nc.tensor.matmul(out, hid[:, u % 2, s * P:(s + 1) * P], m.w2_pair[:, :], start=False, stop=True)
                last.then_inc(hid_used, 1)

            def sums(i, u, blk):
                pe.wait_ge(tile_ready, i * GROUP + (u + 1))
                pe.wait_ge(low_ready, i * GROUP + (u + 1))
                for s in range(u * SUBS, (u + 1) * SUBS):
                    nc.tensor.matmul(flat(by_block[:, bass.ds(blk, 1), :]), oh[:, s, :], msg_src[:, s, :],
                                     start=False, stop=False, skip_group_check=True)
                    last = nc.tensor.matmul(psD[0:BN, 0:BLOCKS * F], dlo[:, s, :],
                                            wide[:, s, :, :].rearrange("p b f -> p (b f)"),
                                            start=False, stop=False, skip_group_check=True)
                last.then_inc(summed, 1)

            def turn(i, summing):
                if summing is not None:
                    sum_blk = blocks_of(pe, m, summing, sum_regs)
                    sums(summing, 0, sum_blk[0])
                    sums(summing, 1, sum_blk[1])
                blk = blocks_of(pe, m, i, regs)
                pe.wait_ge(half_in, i + 1)
                for u in range(GROUP):
                    if u == 2:
                        pe.wait_ge(turn_in, i + 1)
                    hidden(i, u, blk[u])
                    if summing is not None and u in (0, 2):
                        sums(summing, 2 + u // 2, sum_blk[2 + u // 2])
                    if u:
                        reflectors(i, u - 1)
                reflectors(i, GROUP - 1)

            turn(0, None)
            turn(1, None)
            turn(2, None)
            assert (TURNS - 3) % 2 == 0
            with pe.Fori(0, (TURNS - 3) // 2) as k:
                turn(k * 2 + 3, k * 2)
                turn(k * 2 + 4, k * 2 + 1)
            for i in range(TURNS - 3, TURNS):
                sum_blk = blocks_of(pe, m, i, sum_regs)
                for u in range(GROUP):
                    sums(i, u, sum_blk[u])
            nc.tensor.matmul(psD[0:BN, 0:BLOCKS * F], zero[:, 0:BN], zero[:, :], start=False, stop=True,
                             skip_group_check=True).then_inc(d_done, 1)

        @block.scalar
        def _(act):
            act.sem_inc(hid_ready, 2)
            act.sem_inc(x_in, GROUP)
            act.sem_inc(half_in, 1)
            act.sem_inc(turn_in, 1)

            def lows(i):
                nc.scalar.copy(low[:, :], m.meta[:, i * NS:(i + 1) * NS, W_DLO] if isinstance(i, int)
                               else m.meta[:, bass.ds(i * NS, NS), W_DLO]).then_inc(act_step, 1)
                act.wait_ge(act_step, i * (1 + GROUP) + 1)

            def one_hot_low(i, u):
                tile = slice(u * SUBS, (u + 1) * SUBS)
                for s in range(u * SUBS, (u + 1) * SUBS):
                    last = nc.scalar.activation(dist[:, s, :], m.iota[:, 0:BN], ACT.Abs, bias=low[:, s:s + 1], scale=-1.0)
                last.then_inc(act_step, 1)
                act.wait_ge(act_step, i * (1 + GROUP) + (u + 2))
                act.wait_ge(summed, i * GROUP + (u + 1))
                nc.scalar.activation(dlo[:, tile, :], dist[:, tile, :], ACT.Relu, bias=1.0, scale=-1.0).then_inc(low_ready, 1)

            def turn(i, before):
                if before is not None:
                    lows(before)
                for u in range(GROUP):
                    act.wait_ge(z_ready, i * GROUP + (u + 1))
                    act.wait_ge(hid_used, i * GROUP + (u + 1))
                    nc.scalar.activation(hid[:, u % 2, :], psZ[u % 2][:, 0:TILE], ACT.Relu).then_inc(hid_ready, 1)
                    if u == 0:
                        act.wait_ge(turn_in, i + 1)
                    act.wait_ge(gathered[u], i * 32 + 32)
                    tile = slice(u * SUBS, (u + 1) * SUBS)
                    nc.scalar.copy(x_dst[:, tile, :], rows[:, tile, 2 * R1:T1W]).then_inc(x_in, 1)
                    if before is not None:
                        one_hot_low(before, u)
                act.wait_ge(math_done, i + 1)
                act.wait_ge(x_in, i * GROUP + (GROUP + GROUP))
                nc.scalar.copy(xs[:, :, 1, :], x_dst[:, :, :])
                for h, done in ((0, half_in), (1, turn_in)):
                    act.wait_ge(hid_used, i * GROUP + (2 * h + 2 + 2))
                    act.wait_ge(z_done, i * GROUP + (2 * h + 2 + GROUP))
                    slots = slice(h * HALF, (h + 1) * HALF)
                    nc.scalar.copy(xs[:, slots, 0, :], psX[h][:, 0:HALF * (F + 1)].rearrange("p (s f) -> p s f", s=HALF))
                    nc.scalar.copy(vu[:, slots, :, :], psV[h][:, 0:HALF * 2 * F].rearrange("p (s q f) -> p s q f", s=HALF, q=2))\
                        .then_inc(done, 1)

            turn(0, None)
            turn(1, None)
            with act.Fori(2, TURNS) as i:
                turn(i, i - 2)
            for i in (TURNS - 2, TURNS - 1):
                lows(i)
                for u in range(GROUP):
                    one_hot_low(i, u)

        @block.vector
        def _(dve):
            link = Links(dve, math_step)
            link(nc.vector.memset(zero[:, :], 0.0))
            dve.sem_inc(zeroed, 1)
            dve.sem_inc(math_done, 1)
            PER, first = 17, link.n
            tt, V = nc.vector.tensor_tensor, nc.vector

            def spread(a):
                return a.unsqueeze(3).to_broadcast(PAIR)

            def reflect(i, building):
                dve.wait_ge(turn_in, i + 2)
                link(tt(prod[:, :, :, :], vu[:, :, :, :], vu[:, :, :, :], ALU.mult), building)
                link(V.tensor_reduce(rcp[:, :, :], prod[:, :, :, :], AX, ALU.add), building)
                link(V.tensor_scalar(rcp[:, :, :], rcp[:, :, :], 1e-24, 0.5, ALU.max, ALU.mult), building)
                link(V.reciprocal(rcp[:, :, :], rcp[:, :, :]), building)
                link(tt(prod[:, :, :, :], vu[:, :, :, :], xs[:, :, :, 0:F], ALU.mult), building)
                link(V.tensor_reduce(dots[:, :, :], prod[:, :, :, :], AX, ALU.add), building)
                link(tt(dots[:, :, :], dots[:, :, :], rcp[:, :, :], ALU.mult), building)
                link(tt(prod[:, :, :, :], vu[:, :, :, :], spread(dots[:, :, :]), ALU.mult), building)
                for q in range(2):
                    last = tt(w[:, :, 1 - q, :], xs[:, :, q, 0:F], prod[:, :, q, :], ALU.subtract)
                link(last, building)
                link(tt(prod[:, :, :, :], vu[:, :, :, :], w[:, :, :, :], ALU.mult), building)
                link(V.tensor_reduce(dots[:, :, :], prod[:, :, :, :], AX, ALU.add), building)
                link(tt(dots[:, :, :], dots[:, :, :], rcp[:, :, :], ALU.mult), building)
                link(tt(prod[:, :, :, :], vu[:, :, :, :], spread(dots[:, :, :]), ALU.mult), building)
                tt(coef[:, :], xs[:, :, 0, F], xs[:, :, 1, F], ALU.mult)
                link(tt(w[:, :, :, :], w[:, :, :, :], prod[:, :, :, :], ALU.subtract), building)
                for _ in building:
                    pass
                if not isinstance(i, int):
                    dve.wait_ge(tile_ready, i * GROUP)
                link(tt(msg[:, :, :, :], w[:, :, :, :],
                        coef[:, :].unsqueeze(2).unsqueeze(3).to_broadcast(PAIR), ALU.mult))
                dve.sem_inc(math_done, 1)
                link(V.tensor_copy(rec[:, :, :], m.meta[:, i * NS:(i + 1) * NS, :] if isinstance(i, int)
                                   else m.meta[:, bass.ds(i * NS, NS), :]))
                link(tt(dhi[:, :, :], m.iota[:, 0:BLOCKS].unsqueeze(1).to_broadcast([P, NS, BLOCKS]),
                        rec[:, :, W_DHI].unsqueeze(2).to_broadcast([P, NS, BLOCKS]), ALU.is_equal))

            def build(i):
                for u in range(GROUP):
                    yield from build_tile(i, u)

            def build_tile(i, u):
                dve.wait_ge(summed, i * GROUP + (u + 1))
                tile = slice(u * SUBS, (u + 1) * SUBS)
                nc.vector.tensor_copy(msg_src[:, tile, :], msg[:, tile, 0, :])
                one_hots(nc, m, rec[:, tile, :], oh[:, tile, :])
                yield
                for s in range(u * SUBS, (u + 1) * SUBS):
                    last = tt(wide[:, s, :, :], dhi[:, s, :].unsqueeze(2).to_broadcast([P, BLOCKS, F]),
                              msg[:, s, 1, :].unsqueeze(1).to_broadcast([P, BLOCKS, F]), ALU.mult)
                    if s % SUBS == SUBS - 1:
                        last.then_inc(tile_ready, 1)
                    yield

            def turn(i, building):
                link.base, link.n = i * PER + first, 0
                reflect(i, building)
                assert link.n == PER, link.n

            turn(0, iter(()))
            with dve.Fori(1, TURNS) as i:
                turn(i, build(i - 1))
            for _ in build(TURNS - 1):
                pass
            link.base, link.n = first + PER * TURNS, 0
            dve.wait_ge(d_done, 1)
            link(nc.vector.tensor_copy(m.acc[:, :, 0:F],
                                       psD[0:BN, 0:BLOCKS * F].rearrange("p (b f) -> p b f", b=BLOCKS)))


def load_chunks(nc, sp, m, ohT, chunk_in, used, atT=None):
    with sp.Fori(0, TURNS) as i:
        for h in range(2):
            sp.wait_ge(used, i * GROUP + (2 * h + 2))
            cols = slice(h * 2 * TILE, (h + 1) * 2 * TILE)
            sp.dma_start(ohT[:, cols], m.ohT[bass.ds(i, 1), :, cols].rearrange("o p c -> (o p) c")).then_inc(chunk_in[h], 16)
            if atT is not None:
                sp.dma_start(atT[:, cols],
                             m.atT[bass.ds(i, 1), :, cols].rearrange("o p c -> (o p) c")).then_inc(chunk_in[h], 16)


def residual_norm(nc, m, name, add, relu=False):
    with Stage(name) as ctx:
        sq = sb(nc, ctx, "squares", [BN, BLOCKS, F])
        st = sb(nc, ctx, "row_stats", [BN, 3, BLOCKS])
        var_ready, root_ready, step = sems(nc, ctx, "var_ready root_ready norm_step")
        block = ctx.enter_context(nc.Block())

        @block.vector
        def _(dve):
            link = Links(dve, step)
            if relu:
                link(nc.vector.tensor_tensor(sq[:, :, :], m.x[:, :, :], add[:, :, 0:F], ALU.add))
                link(nc.vector.tensor_scalar(sq[:, :, :], sq[:, :, :], 0.0, None, ALU.max))
                link(nc.vector.tensor_tensor(m.x[:, :, :], m.x[:, :, :], sq[:, :, :], ALU.add))
            else:
                link(nc.vector.tensor_tensor(m.x[:, :, :], m.x[:, :, :], add[:, :, 0:F], ALU.add))
            norm_steps(nc, dve, link, m, m.x[:, :, :], sq[:, :, :], st, var_ready, root_ready)

        @block.scalar
        def _(act):
            root(nc, act, st[:, 2, :], var_ready, root_ready)


def conv_nodes_in(nc, m, name, w_dram, x_in):
    with Stage(name) as ctx:
        wt = sb(nc, ctx, "weight", [F, F])
        xT = sb(nc, ctx, "xT", [F, N])
        rest = sb(nc, ctx, "rest", [BN, BLOCKS, F])
        pT = [bank(nc, ctx, f"xT_psum{k}") for k in range(2)]
        pW = bank(nc, ctx, "project_psum")
        w_in, deg_ready, deg_root, transposed, copied, projected, step = sems(
            nc, ctx, "w_in deg_ready deg_root xT_psum_ready xT_ready projected step")
        block = ctx.enter_context(nc.Block())

        @block.sync
        def _(sp):
            sp.dma_start(wt[:, :], w_dram).then_inc(w_in, 16)

        @block.tensor
        def _(pe):
            transpose_nodes(nc, pe, m, x_in, F, pT, xT, transposed, copied)
            pe.wait_ge(w_in, 16)
            pe.wait_ge(copied, -(-BLOCKS // 4))
            for b in range(BLOCKS):
                last = nc.tensor.matmul(pW[0:BN, b * F:(b + 1) * F], xT[:, b * BN:(b + 1) * BN], wt[:, :],
                                        start=True, stop=True)
            last.then_inc(projected, 1)

        @block.scalar
        def _(act):
            act.wait_ge(deg_ready, 1)
            nc.scalar.activation(m.dinv[:, :], m.dinv[:, :], ACT.Sqrt).then_inc(deg_root, 1)
            copy_transposed(nc, act, F, pT, xT, transposed, copied)

        @block.vector
        def _(dve):
            link = Links(dve, step)
            nc.vector.tensor_scalar(m.dinv[:, :], m.deg_dst[:, :], 1.0, None, ALU.add).then_inc(deg_ready, 1)
            dve.wait_ge(deg_root, 1)
            link(nc.vector.reciprocal(m.dinv[:, :], m.dinv[:, :]))
            dve.wait_ge(projected, 1)
            link(nc.vector.tensor_tensor(m.scaled[:, :, :], pW[0:BN, 0:BLOCKS * F].rearrange("p (b f) -> p b f", b=BLOCKS),
                                         m.dinv[:, :].unsqueeze(2).to_broadcast([BN, BLOCKS, F]), ALU.mult))
            split3(nc, link, tuple(m.rows2[:, :, k, :] for k in range(3)), m.scaled[:, :, :], rest[:, :, :])


def conv_edges(nc, m, name, b_dram, out, last_conv):
    with Stage(name) as ctx:
        ohT = sb(nc, ctx, "one_hot_chunk", [BN, GROUP * TILE], BF16)
        low = sb(nc, ctx, "dst_low", [P, NS])
        high = sb(nc, ctx, "dst_high", [P, NS])
        dlo = sb(nc, ctx, "one_hot_dst_low", [P, NS, BN])
        dhi = sb(nc, ctx, "one_hot_dst_high", [P, NS, BLOCKS])
        wide = sb(nc, ctx, "rows_by_block", [P, NS, BLOCKS, F])
        zero = sb(nc, ctx, "zero_square", [P, BLOCKS * F], BF16)
        bias = sb(nc, ctx, "bias", [BN, F])
        psG = [bank(nc, ctx, f"row_psum{k}") for k in range(2)]
        psD = bank(nc, ctx, "sum_psum")
        (b_in, chunk0, chunk1, low_step, hot_ready, fetched, spread_done, summed, zeroed, d_done, step) = sems(
            nc, ctx, "b_in chunk_in0 chunk_in1 low_step hot_ready fetched spread_done summed zeroed d_done step")
        chunk_in = (chunk0, chunk1)
        block = ctx.enter_context(nc.Block())

        @block.sync
        def _(sp):
            sp.dma_start(bias[:, :], b_dram.rearrange("(o f) -> o f", o=1).to_broadcast([BN, F])).then_inc(b_in, 16)
            load_chunks(nc, sp, m, ohT, chunk_in, fetched)

        @block.gpsimd
        def _(gp):
            with gp.Fori(0, TURNS) as i:
                for h in range(2):
                    gp.wait_ge(summed, i * GROUP + (2 * h + 2))
                    gp.sem_inc(m.pool_steps, 1)
                    half = slice(h * NS // 2, (h + 1) * NS // 2)
                    nc.gpsimd.tensor_copy(low[:, half], m.meta[:, bass.ds(i * NS + h * (NS // 2), NS // 2), W_DLO])\
                        .then_inc(low_step, 1)
                    gp.wait_ge(low_step, i * 2 + (h + 1))
                    gp.sem_inc(m.pool_steps, 1)
                    for u in (2 * h, 2 * h + 1):
                        for s in range(u * SUBS, (u + 1) * SUBS):
                            last = nc.gpsimd.tensor_scalar(dlo[:, s, :], m.iota[:, 0:BN], low[:, s:s + 1], None, ALU.is_equal)
                        last.then_inc(hot_ready, 1)

        @block.tensor
        def _(pe):
            pe.sem_inc(fetched, GROUP)
            pe.sem_inc(summed, GROUP)
            pe.wait_ge(zeroed, 1)
            nc.tensor.matmul(psD[0:BN, 0:BLOCKS * F], zero[:, 0:BN], zero[:, :], start=True, stop=False,
                             skip_group_check=True)

            regs = [pe.alloc_register(f"{name}_block_of_tile{u}") for u in range(GROUP)]

            def fetch(i, u, blk):
                pe.wait_ge(spread_done, i * GROUP + (u + 1))
                if u % 2 == 0:
                    pe.wait_ge(chunk_in[u // 2], i * 16 + 16)
                for s in range(SUBS):
                    for k in range(3):
                        c = (u * SUBS + s) * P
                        last = nc.tensor.matmul(psG[u % 2][:, s * F:(s + 1) * F], ohT[:, c:c + P],
                                                flat(m.rows2[:, bass.ds(blk, 1), k, :]), start=(k == 0), stop=(k == 2))
                last.then_inc(fetched, 1)

            def sums(i, u):
                pe.wait_ge(spread_done, i * GROUP + (u + 1 + 2))
                pe.wait_ge(hot_ready, i * GROUP + (u + 1))
                for s in range(SUBS):
                    last = nc.tensor.matmul(psD[0:BN, 0:BLOCKS * F], dlo[:, u * SUBS + s, :],
                                            wide[:, u * SUBS + s, :, :].rearrange("p b f -> p (b f)"),
                                            start=False, stop=False, skip_group_check=True)
                last.then_inc(summed, 1)

            blk = blocks_of(pe, m, 0, regs)
            for u in range(GROUP):
                fetch(0, u, blk[u])
                if u:
                    sums(0, u - 1)
            with pe.Fori(1, TURNS) as i:
                blk = blocks_of(pe, m, i, regs)
                for u in range(GROUP):
                    fetch(i, u, blk[u])
                    sums(i if u else i - 1, (u - 1) % GROUP)
            sums(TURNS - 1, GROUP - 1)
            nc.tensor.matmul(psD[0:BN, 0:BLOCKS * F], zero[:, 0:BN], zero[:, :], start=False, stop=True,
                             skip_group_check=True).then_inc(d_done, 1)

        @block.vector
        def _(dve):
            link = Links(dve, step)
            nc.vector.memset(zero[:, :], 0.0).then_inc(zeroed, 1)
            dve.sem_inc(spread_done, 2)
            with dve.Fori(0, TURNS) as i:
                link.base, link.n = i * 2, 0
                link(nc.vector.tensor_copy(high[:, :], m.meta[:, bass.ds(i * NS, NS), W_DHI]))
                link(nc.vector.tensor_tensor(dhi[:, :, :], m.iota[:, 0:BLOCKS].unsqueeze(1).to_broadcast([P, NS, BLOCKS]),
                                             high[:, :].unsqueeze(2).to_broadcast([P, NS, BLOCKS]), ALU.is_equal))
                for u in range(GROUP):
                    dve.wait_ge(fetched, i * GROUP + (u + 1 + GROUP))
                    dve.wait_ge(summed, i * GROUP + (u + 1))
                    for s in range(SUBS):
                        last = nc.vector.tensor_tensor(
                            wide[:, u * SUBS + s, :, :],
                            psG[u % 2][:, s * F:(s + 1) * F].unsqueeze(1).to_broadcast([P, BLOCKS, F]),
                            dhi[:, u * SUBS + s, :].unsqueeze(2).to_broadcast([P, BLOCKS, F]), ALU.mult)
                    last.then_inc(spread_done, 1)
            link.base, link.n = 2 * TURNS, 0
            dve.wait_ge(d_done, 1)
            dve.wait_ge(b_in, 16)
            full = [BN, BLOCKS, F]
            link(nc.vector.tensor_tensor(out[:, :, :], psD[0:BN, 0:BLOCKS * F].rearrange("p (b f) -> p b f", b=BLOCKS),
                                         m.scaled[:, :, :], ALU.add))
            link(nc.vector.tensor_tensor(out[:, :, :], out[:, :, :], m.dinv[:, :].unsqueeze(2).to_broadcast(full), ALU.mult))
            link(nc.vector.tensor_tensor(out[:, :, :], out[:, :, :], bias[:, :].unsqueeze(1).to_broadcast(full), ALU.add))
            if not last_conv:
                link(nc.vector.tensor_scalar(out[:, :, :], out[:, :, :], 0.0, None, ALU.max))


CHUNK = 500
CHUNKS = [(c, min(CHUNK, N - c)) for c in range(0, N, CHUNK)]


def embed(nc, m, w):
    with Stage("embed") as ctx:
        wt = sb(nc, ctx, "weight", [F, HID])
        bt = sb(nc, ctx, "bias", [HID, 1])
        xT = sb(nc, ctx, "xT", [F, N])
        pT = [bank(nc, ctx, f"xT_psum{k}") for k in range(2)]
        pH = [bank(nc, ctx, f"h_psum{k}") for k in range(2)]
        w_in, transposed, copied, projected, stored = sems(nc, ctx, "w_in xT_psum_ready xT_ready projected stored")
        block = ctx.enter_context(nc.Block())

        @block.sync
        def _(sp):
            sp.dma_start(wt[:, :], w["L3_gnn_emb_w"]).then_inc(w_in, 16)
            sp.dma_start(bt[:, :], w["L3_gnn_emb_b"].rearrange("(h o) -> h o", o=1)).then_inc(w_in, 16)
            sp.dma_start(m.node_mask[:, :], w["node_vec1"].rearrange("n o -> o n").to_broadcast([HID, N])).then_inc(w_in, 16)

        @block.tensor
        def _(pe):
            transpose_nodes(nc, pe, m, m.x, F, pT, xT, transposed, copied)
            pe.wait_ge(w_in, 48)
            pe.wait_ge(copied, -(-BLOCKS // 4))
            for k, (c, n) in enumerate(CHUNKS):
                if k >= 2:
                    pe.wait_ge(stored, k - 1)
                nc.tensor.matmul(pH[k % 2][:, 0:n], wt[:, :], xT[:, c:c + n], start=True, stop=True).then_inc(projected, 1)

        @block.scalar
        def _(act):
            copy_transposed(nc, act, F, pT, xT, transposed, copied)

        @block.vector
        def _(dve):
            for k, (c, n) in enumerate(CHUNKS):
                dve.wait_ge(projected, k + 1)
                nc.vector.tensor_scalar(m.h[:, c:c + n], pH[k % 2][:, 0:n], bt[:, 0:1], None, ALU.add).then_inc(stored, 1)


def egnn_layers(nc, m, w):
    W_DMAS = 6 + 9 + 3
    with Stage("egnn") as ctx:
        w_ab = sb(nc, ctx, "edge_w1_nodes", [HID, 2, HID])
        w_c = sb(nc, ctx, "edge_w1_attr", [AP9, HID])
        wc_tmp = sb(nc, ctx, "edge_w1_attr_whole_parts", [AP9, 3, HID], BF16)
        wc_parts = sb(nc, ctx, "edge_w1_attr_parts", [AP9, HID], BF16)
        w_2 = sb(nc, ctx, "edge_w2", [HID, HID])
        n_1 = sb(nc, ctx, "node_w1", [HID, 2, HID])
        n_2 = sb(nc, ctx, "node_w2", [HID, HID])
        biases = sb(nc, ctx, "biases", [HID, 3])
        rows = sb(nc, ctx, "rows_of_src_parts", [BN, BLOCKS, 3, HID], BF16)
        rest = sb(nc, ctx, "rest", [BN, HID])
        q_sb = sb(nc, ctx, "rows_of_dst", [BN, BLOCKS, HID])
        agg = sb(nc, ctx, "sums", [HID, N])
        n_hid = sb(nc, ctx, "node_hidden", [HID, 2, CHUNK])
        idx = [sb(nc, ctx, f"index_buf{b}", [P, NS], I32) for b in range(2)]
        q_got = [sb(nc, ctx, f"rows_gathered{b}", [P, NS, HID]) for b in range(2)]
        ohT = sb(nc, ctx, "one_hot_chunk", [BN, GROUP * TILE], BF16)
        atT = sb(nc, ctx, "attr_chunk", [AP9, GROUP * TILE], BF16)
        rec = sb(nc, ctx, "turn_records", [P, NS, PW])
        hid = sb(nc, ctx, "hidden", [HID, 2, TILE])
        ef = sb(nc, ctx, "edge_features", [P, 2, SUBS, HID])
        oh = sb(nc, ctx, "one_hot_weighted", [P, 2 * SUBS, BN])
        psZ = [bank(nc, ctx, f"hidden_psum{k}") for k in range(2)]
        psY = [bank(nc, ctx, f"feature_psum{k}") for k in range(2)]
        psS = [bank(nc, ctx, f"sum_psum{k}") for k in range(2)]
        (w_nodes_in, w_in, w_split, projected, q_projected, kept, q_kept, q_out, layer_done, idx_ready, chunk0, chunk1, z_done,
         hid_ready, hid_used, ef_ready, summed, added, hot_ready, edges_done, n1_done, n_silu, n2_done, updated, step, gates) = sems(
            nc, ctx, "w_nodes_in w_in w_split projected q_projected kept q_kept q_out layer_done idx_ready chunk_in0 "
            "chunk_in1 z_done hid_ready hid_used ef_ready summed added hot_ready edges_done n1_done n_silu n2_done "
            "updated step gates")
        gathered = (pool_dma_sems(nc, ctx, "gathered00 gathered01 gathered02 gathered03"),
                    pool_dma_sems(nc, ctx, "gathered10 gathered11 gathered12 gathered13"))
        chunk_in = (chunk0, chunk1)
        block = ctx.enter_context(nc.Block())
        NC = len(CHUNKS)

        USES = ((TURNS + 1) // 2, TURNS // 2)
        assert TURNS % 2 == 1

        def in_turn(eng, f):
            f(0, 0, 0)
            eng.sem_inc(gates, 1)
            with eng.Fori(0, TURNS // 2) as k:
                f(k * 2 + 1, 1, k)
                f(k * 2 + 2, 0, k + 1)

        def pipeline(eng, steps):
            def turn(i, b, n):
                for u in range(GROUP):
                    for lag, f in enumerate(steps):
                        if lag == 0:
                            f(i, u, b, n)
                        elif u >= lag:
                            f(i, u - lag)
                        elif not isinstance(i, int):
                            f(i - 1, u - lag + GROUP)
            in_turn(eng, turn)
            for u in range(GROUP, GROUP + len(steps) - 1):
                for lag, f in enumerate(steps):
                    if u - lag < GROUP:
                        f(TURNS - 1, u - lag)

        @block.sync
        def _(sp):
            with sp.Fori(0, LAYERS) as l:
                sp.wait_ge(layer_done, l + 1)
                one = bass.ds(l, 1)
                w1, nw1 = w["L3_gnn_edge_w1"], w["L3_gnn_node_w1"]
                for k in range(2):
                    sp.dma_start(w_ab[:, k, :], w1[one, k * HID:(k + 1) * HID, :].rearrange("o k h -> (o k) h"))\
                        .then_inc(w_nodes_in, 16)
                for r in range(9):
                    sp.dma_start(w_c[r * EA:(r + 1) * EA, :],
                                 w1[one, 2 * HID:2 * HID + EA, :].rearrange("o k h -> (o k) h")).then_inc(w_in, 16)
                for r in range(3):
                    sp.dma_start(m.b2_rows[r:r + 1, :], w["L3_gnn_edge_b2"][one, :]).then_inc(w_in, 16)
                sp.dma_start(w_2[:, :], w["L3_gnn_edge_w2"][one, :, :].rearrange("o k h -> (o k) h")).then_inc(w_in, 16)
                sp.dma_start(n_1[:, :, :], nw1[one, :, :].rearrange("o (a k) h -> k (o a) h", a=2)).then_inc(w_in, 16)
                sp.dma_start(n_2[:, :], w["L3_gnn_node_w2"][one, :, :].rearrange("o k h -> (o k) h")).then_inc(w_in, 16)
                sp.dma_start(biases[:, 0:1], w["L3_gnn_edge_b1"][one, :].rearrange("o h -> h o")).then_inc(w_in, 16)
                sp.dma_start(biases[:, 1:2], w["L3_gnn_node_b1"][one, :].rearrange("o h -> h o")).then_inc(w_in, 16)
                sp.dma_start(biases[:, 2:3], w["L3_gnn_node_b2"][one, :].rearrange("o h -> h o")).then_inc(w_in, 16)
                sp.wait_ge(q_kept, l * BLOCKS + (BLOCKS + 2))
                sp.dma_start(m.tab3.rearrange("(b p) f -> p b f", p=BN), q_sb[:, :, :]).then_inc(q_out, 16)
                with sp.Fori(0, TURNS) as i:
                    for h in range(2):
                        sp.wait_ge(z_done, l * TILES + i * GROUP + (2 * h + 2 + GROUP))
                        cols = slice(h * 2 * TILE, (h + 1) * 2 * TILE)
                        sp.dma_start(ohT[:, cols], m.ohT[bass.ds(i, 1), :, cols].rearrange("o p c -> (o p) c"))\
                            .then_inc(chunk_in[h], 16)
                        sp.dma_start(atT[:, cols], m.atT[bass.ds(i, 1), :, cols].rearrange("o p c -> (o p) c"))\
                            .then_inc(chunk_in[h], 16)

        @block.gpsimd
        def _(gp):
            with gp.Fori(0, LAYERS) as l:
                gp.wait_ge(q_out, l * 16 + 16)
                gp.sem_inc(m.pool_steps, 1)
                def turn(i, b):
                    gather_turn(nc, gp, m, i, idx[b], q_got[b], m.tab3, gathered[b], z_done, idx_ready, l * TILES, l * TURNS)

                turn(0, 0)
                with gp.Fori(0, TURNS // 2) as k:
                    turn(k * 2 + 1, 1)
                    turn(k * 2 + 2, 0)

        @block.tensor
        def _(pe):
            pe.sem_inc(z_done, 2 * GROUP)
            regs = [pe.alloc_register(f"egnn_block_of_tile{u}") for u in range(GROUP)]
            blk = []
            pe.sem_inc(hid_used, 2)
            pe.sem_inc(summed, 2)
            with pe.Fori(0, LAYERS) as l:
                pe.wait_ge(w_nodes_in, l * 32 + 32)
                pe.wait_ge(updated, l * NC + NC)
                for b in range(BLOCKS):
                    pe.wait_ge(q_kept, l * BLOCKS + (b + 1))
                    nc.tensor.matmul(psY[b % 2][0:BN, 0:HID], m.h[:, b * BN:(b + 1) * BN], w_ab[:, 1, :],
                                     start=True, stop=True).then_inc(q_projected, 1)
                for b in range(BLOCKS):
                    pe.wait_ge(kept, l * BLOCKS + (b + 1))
                    nc.tensor.matmul(psZ[b % 2][0:BN, 0:HID], m.h[:, b * BN:(b + 1) * BN], w_ab[:, 0, :],
                                     start=True, stop=True).then_inc(projected, 1)
                pe.wait_ge(kept, l * BLOCKS + (BLOCKS + 2))
                pe.wait_ge(q_kept, l * BLOCKS + (BLOCKS + 2))
                pe.wait_ge(w_split, l + 1)
                pe.sem_inc(gates, 1)

                def hidden(i, u, b, n):
                    t = l * TILES + i * GROUP
                    if u == 0:
                        blk[:] = blocks_of(pe, m, i, regs)
                    pe.wait_ge(hid_ready, t + (u + 1))
                    cols = slice(u * TILE, (u + 1) * TILE)
                    if u % 2 == 0:
                        pe.wait_ge(chunk_in[u // 2], l * (32 * TURNS) + (i * 32 + 32))
                    out = psZ[u % 2][:, 0:TILE]
                    nc.tensor.matmul(out, wc_parts[:, :], atT[:, cols], start=True, stop=False, skip_group_check=True)
                    for k in range(3):
                        nc.tensor.matmul(out, flat(rows[:, bass.ds(blk[u], 1), k, :]), ohT[:, cols], start=False, stop=False,
                                         skip_group_check=True)
                    pe.wait_ge(gathered[b][u], l * (32 * USES[b]) + (n * 32 + 32))
                    for s in range(SUBS):
                        last = nc.tensor.matmul(psZ[u % 2][:, s * P:(s + 1) * P], q_got[b][:, u * SUBS + s, :], m.ident[:, :],
                                                start=False, stop=(s == SUBS - 1), is_transpose=True, skip_group_check=True)
                    last.then_inc(z_done, 1)

                def features(i, u):
                    t = l * TILES + i * GROUP
                    pe.wait_ge(ef_ready, t + (u + 1))
                    pe.wait_ge(hid_ready, t + (u + 1 + 2))
                    for s in range(SUBS):
                        out = psY[u % 2][:, s * HID:(s + 1) * HID]
                        nc.tensor.matmul(out, m.ones3[:, :], m.b2_parts[:, :], start=True, stop=False)
                        last = nc.tensor.matmul(out, hid[:, u % 2, s * P:(s + 1) * P], w_2[:, :], start=False, stop=True)
                    last.then_inc(hid_used, 1)

                def sums(i, u):
                    t = l * TILES + i * GROUP
                    pe.wait_ge(added, t + (u + 1))
                    pe.wait_ge(hot_ready, t + (u + 1))
                    pe.wait_ge(ef_ready, t + (u + 1 + 2))
                    for s in range(SUBS):
                        last = nc.tensor.matmul(psS[u % 2][:, 0:BN], ef[:, u % 2, s, :], oh[:, (u % 2) * SUBS + s, :],
                                                start=(s == 0), stop=(s == SUBS - 1))
                    last.then_inc(summed, 1)

                pipeline(pe, (hidden, features, sums))
                pe.wait_ge(edges_done, l + 1)
                def node_hidden(k):
                    c, n = CHUNKS[k]
                    pe.wait_ge(n_silu, l * NC + (k + 1))
                    for a, v in enumerate((m.h, agg)):
                        last = nc.tensor.matmul(psZ[k % 2][:, 0:n], n_1[:, a, :], v[:, c:c + n], start=(a == 0), stop=(a == 1))
                    last.then_inc(n1_done, 1)

                def node_out(k):
                    n = CHUNKS[k][1]
                    pe.wait_ge(n_silu, l * NC + (k + 1 + 2))
                    if k >= 2:
                        pe.wait_ge(updated, l * NC + (NC + k - 1))
                    nc.tensor.matmul(psY[k % 2][:, 0:n], n_2[:, :], n_hid[:, k % 2, 0:n], start=True, stop=True)\
                        .then_inc(n2_done, 1)

                node_hidden(0)
                for k in range(1, NC):
                    node_hidden(k)
                    node_out(k - 1)
                node_out(NC - 1)

        @block.scalar
        def _(act):
            act.sem_inc(hid_ready, 2)
            act.sem_inc(ef_ready, 2)
            act.sem_inc(n_silu, 2)
            act.sem_inc(q_kept, 2)
            with act.Fori(0, LAYERS) as l:
                for b in range(BLOCKS):
                    act.wait_ge(q_projected, l * BLOCKS + (b + 1))
                    if b == 0:
                        act.wait_ge(layer_done, l + 1)
                    nc.scalar.copy(q_sb[:, b, :], psY[b % 2][0:BN, 0:HID]).then_inc(q_kept, 1)

                def hidden(i, u, b, n):
                    t = l * TILES + i * GROUP
                    act.wait_ge(z_done, t + (u + 1 + 2 * GROUP))
                    act.wait_ge(hid_used, t + (u + 1))
                    nc.scalar.activation(hid[:, u % 2, :], psZ[u % 2][:, 0:TILE], ACT.Silu, bias=biases[:, 0:1])\
                        .then_inc(hid_ready, 1)

                def features(i, u):
                    t = l * TILES + i * GROUP
                    act.wait_ge(hid_used, t + (u + 1 + 2))
                    act.wait_ge(summed, t + (u + 1))
                    nc.scalar.activation(ef[:, u % 2, :, :].rearrange("p s h -> p (s h)"), psY[u % 2][:, 0:SUBS * HID],
                                         ACT.Silu).then_inc(ef_ready, 1)

                pipeline(act, (hidden, features))
                for k, (c, n) in enumerate(CHUNKS):
                    act.wait_ge(n1_done, l * NC + (k + 1))
                    if k >= 2:
                        act.wait_ge(n2_done, l * NC + (k - 1))
                    nc.scalar.activation(n_hid[:, k % 2, 0:n], psZ[k % 2][:, 0:n], ACT.Silu, bias=biases[:, 1:2])\
                        .then_inc(n_silu, 1)

        @block.vector
        def _(dve):
            dve.sem_inc(added, 2)
            dve.sem_inc(kept, 2)
            dve.sem_inc(updated, NC)
            dve.sem_inc(layer_done, 1)
            LAYER_STEPS = 14 + 4 * BLOCKS + NC + TURNS
            with dve.Fori(0, LAYERS) as l:
                link = Links(dve, step)
                link.base = l * LAYER_STEPS
                dve.wait_ge(w_in, l * (16 * W_DMAS) + 16 * W_DMAS)
                split_rows(nc, link, wc_parts[:, :], w_c[:, :], m.row_masks[:, :], *(wc_tmp[:, k, :] for k in range(3)), w_c[:, :])
                split_rows(nc, link, m.b2_parts[:, :], m.b2_rows[:, :], m.ident[0:3, 0:3],
                           *(m.b2_tmp[:, k, :] for k in range(3)), m.b2_rows[:, :])
                dve.sem_inc(w_split, 1)
                for b in range(BLOCKS):
                    dve.wait_ge(projected, l * BLOCKS + (b + 1))
                    split3(nc, link, tuple(rows[:, b, k, :] for k in range(3)), psZ[b % 2][0:BN, 0:HID], rest[:, :])
                    dve.sem_inc(kept, 1)
                nc.vector.memset(agg[:, :], 0.0)

                def build(i, u, b, n):
                    t = l * TILES + i * GROUP
                    if u == 0:
                        ins = nc.vector.tensor_copy(rec[:, :, :], m.meta[:, i * NS:(i + 1) * NS, :] if isinstance(i, int)
                                                    else m.meta[:, bass.ds(i * NS, NS), :])
                        ins.then_inc(step, 1)
                        dve.wait_ge(step, l * LAYER_STEPS + (14 + 4 * BLOCKS) + (i + 1))
                    dve.wait_ge(summed, t + (u + 1))
                    for s in range(SUBS):
                        r = rec[:, u * SUBS + s, :]
                        last = nc.vector.tensor_scalar(oh[:, (u % 2) * SUBS + s, :], m.iota[:, 0:BN], r[:, W_REL:W_REL + 1],
                                                       r[:, W_EW:W_EW + 1], ALU.is_equal, ALU.mult)
                    last.then_inc(hot_ready, 1)

                def add(i, u):
                    t = l * TILES + i * GROUP
                    blk = block_of(dve, m, i, u)
                    dve.wait_ge(summed, t + (u + 1 + 2))
                    to = agg[:, bass.ds(blk * BN, BN)]
                    nc.vector.tensor_tensor(to, to, psS[u % 2][:, 0:BN], ALU.add).then_inc(added, 1)
                    dve.wait_ge(added, t + (u + 1 + 2))

                pipeline(dve, (build, add))
                dve.sem_inc(edges_done, 1)
                link.base = l * LAYER_STEPS + (14 + 4 * BLOCKS) + TURNS
                link.n = 0
                for k, (c, n) in enumerate(CHUNKS):
                    dve.wait_ge(n2_done, l * NC + (k + 1))
                    h = m.h[:, c:c + n]
                    link(nc.vector.scalar_tensor_tensor(h, psY[k % 2][:, 0:n], biases[:, 2:3], h, ALU.add, ALU.add))
                    nc.vector.tensor_tensor(h, h, m.node_mask[:, c:c + n], ALU.mult).then_inc(updated, 1)
                dve.wait_ge(updated, l * NC + 2 * NC)
                dve.sem_inc(layer_done, 1)


def read_out(nc, m, w, out):
    with Stage("read_out") as ctx:
        wt = sb(nc, ctx, "weight", [HID, F])
        bt = sb(nc, ctx, "bias", [BN, F])
        mask = sb(nc, ctx, "mask", [BN, BLOCKS])
        o = sb(nc, ctx, "out", [BN, BLOCKS, F])
        sq = sb(nc, ctx, "squares", [BN, BLOCKS, F])
        st = sb(nc, ctx, "row_stats", [BN, 3, BLOCKS])
        ps = bank(nc, ctx, "psum")
        w_in, projected, var_ready, root_ready, step, done, out_done = sems(
            nc, ctx, "w_in projected var_ready root_ready step norm_done out_done")
        block = ctx.enter_context(nc.Block())

        @block.sync
        def _(sp):
            sp.dma_start(wt[:, :], w["L3_gnn_out_w"]).then_inc(w_in, 16)
            sp.dma_start(bt[:, :], w["L3_gnn_out_b"].rearrange("(o f) -> o f", o=1).to_broadcast([BN, F])).then_inc(w_in, 16)
            with nc.allow_non_contiguous_dma(reason="the node mask, node by node, once"):
                sp.dma_start(mask[:, :], w["node_vec1"].rearrange("(b p) o -> p (b o)", p=BN)).then_inc(w_in, 16)
            sp.wait_ge(done, 1)
            sp.dma_start(out.rearrange("(b p) f -> p b f", p=BN), m.x[:, :, :]).then_inc(out_done, 16)
            sp.wait_ge(out_done, 16)

        @block.tensor
        def _(pe):
            pe.wait_ge(w_in, 48)
            for b in range(BLOCKS):
                last = nc.tensor.matmul(ps[0:BN, b * F:(b + 1) * F], m.h[:, b * BN:(b + 1) * BN], wt[:, :], start=True, stop=True)
            last.then_inc(projected, 1)

        @block.vector
        def _(dve):
            link = Links(dve, step)
            full = [BN, BLOCKS, F]
            dve.wait_ge(projected, 1)
            dve.wait_ge(w_in, 48)
            link(nc.vector.tensor_tensor(o[:, :, :], ps[0:BN, 0:BLOCKS * F].rearrange("p (b f) -> p b f", b=BLOCKS),
                                         bt[:, :].unsqueeze(1).to_broadcast(full), ALU.add))
            link(nc.vector.tensor_tensor(o[:, :, :], o[:, :, :], mask[:, :].unsqueeze(2).to_broadcast(full), ALU.mult))
            link(nc.vector.tensor_tensor(m.x[:, :, :], m.x[:, :, :], o[:, :, :], ALU.add))
            norm_steps(nc, dve, link, m, m.x[:, :, :], sq[:, :, :], st, var_ready, root_ready)
            dve.sem_inc(done, 1)

        @block.scalar
        def _(act):
            root(nc, act, st[:, 2, :], var_ready, root_ready)


def program(nc, t, out):
    m = Mem()
    m.nc = nc
    with Stage("kept") as ctx:
        m.ident = sb(nc, ctx, "ident", [P, P])
        m.row_masks = sb(nc, ctx, "row_masks", [AP9, 3])
        m.iota_i = sb(nc, ctx, "iota_int", [P, P], I32)
        m.iota_t = sb(nc, ctx, "iota_tiles", [1, TILES], I32)
        m.iota = sb(nc, ctx, "iota", [P, P])
        m.tile_block = sb(nc, ctx, "tile_block", [1, TILES], I32)
        m.ones3 = sb(nc, ctx, "ones3", [3, P], BF16)
        m.meta = sb(nc, ctx, "slot_records", [P, NSUB, PW])
        m.x = sb(nc, ctx, "x_nodes", [BN, BLOCKS, F])
        m.acc = sb(nc, ctx, "sums_by_src", [BN, BLOCKS, F + 1])
        m.deg_dst = sb(nc, ctx, "degree_dst", [BN, BLOCKS])
        m.x_in = ctx.enter_context(nc.semaphore("x_in"))
        m.rows1 = sb(nc, ctx, "rows_of_src_parts", [BN, BLOCKS, 3, T1W], BF16)
        m.w2_pair = sb(nc, ctx, "w2_pair", [2 * R1, 2 * F])
        m.b2_rows = sb(nc, ctx, "b2_rows", [3, P])
        m.b2_tmp = sb(nc, ctx, "b2_parts_whole", [3, 3, P], BF16)
        m.b2_parts = sb(nc, ctx, "b2_parts", [3, P], BF16)
        m.conv = sb(nc, ctx, "conv_out", [BN, BLOCKS, F])
        m.scaled = sb(nc, ctx, "conv_scaled", [BN, BLOCKS, F])
        m.rows2 = sb(nc, ctx, "conv_scaled_parts", [BN, BLOCKS, 3, F], BF16)
        m.dinv = sb(nc, ctx, "root_degree", [BN, BLOCKS])
        m.h = sb(nc, ctx, "h", [HID, N])
        m.node_mask = sb(nc, ctx, "node_mask", [HID, N])
        m.tab3 = nc.dram_tensor("egnn_table_of_dst", (N, HID), F32).ap()
        m.tab1 = nc.dram_tensor("sheaf_table_of_dst", (N, T1W), F32).ap()
        m.pool_steps = ctx.enter_context(nc.semaphore("pool_steps"))
        m.slots = nc.dram_tensor("slot_table", (P * ROWC, PW), F32).ap()
        m.ytab = nc.dram_tensor("y_table", (N, F + 1), F32).ap()
        m.ohT = nc.dram_tensor("one_hot_src_T", (TURNS, BN, GROUP * TILE), BF16).ap()
        m.atT = nc.dram_tensor("attr_parts_T", (TURNS, AP9, GROUP * TILE), BF16).ap()
        sort_edges(nc, m, t["src"], t["dst"], t["edge_attr_4"], t["edge_weight1"])
        first_pass(nc, m, t["x"], t["dst"])
        nodes_before_l1(nc, m, t)
        sheaf_edges(nc, m)
        residual_norm(nc, m, "after_l1", m.acc, relu=True)
        conv_nodes_in(nc, m, "conv1_nodes", t["L2_gnn_W1"], m.x)
        conv_edges(nc, m, "conv1_edges", t["L2_gnn_b1"], m.conv, False)
        conv_nodes_in(nc, m, "conv2_nodes", t["L2_gnn_W2"], m.conv)
        conv_edges(nc, m, "conv2_edges", t["L2_gnn_b2"], m.conv, True)
        residual_norm(nc, m, "after_l2", m.conv)
        embed(nc, m, t)
        egnn_layers(nc, m, t)
        read_out(nc, m, t, out)


def kernel(**inputs):
    import concourse.bacc as bacc
    from concourse.bass_utils import run_bass_kernel_spmd as run
    nc = bacc.Bacc("TRN2", target_bir_lowering=False, num_devices=1)
    arrays, t = {}, {}
    for name, a in inputs.items():
        a = np.ascontiguousarray(a)
        arrays["in_" + name] = a
        t[name] = nc.dram_tensor("in_" + name, a.shape, mybir.dt.from_np(a.dtype), kind="ExternalInput").ap()
    out = nc.dram_tensor("out_x", (N, F), F32, kind="ExternalOutput").ap()
    program(nc, t, out)
    return run(nc, [arrays], core_ids=[0]).results[0]["out_x"]
```
